# Optimizing a Trainium2 kernel written in Bass

```python
import numpy as np
import jax
import jax.numpy as jnp

def _softmax(x, axis=-1):
    return jax.nn.softmax(x, axis=axis)
def _gelu(x):
    return jax.nn.gelu(x, approximate=True)
def _silu(x):
    return jax.nn.silu(x)
def _sigmoid(x):
    return jax.nn.sigmoid(x)
def _layernorm(x, axis=-1, eps=1e-5):
    m = jnp.mean(x, axis=axis, keepdims=True)
    v = jnp.var(x, axis=axis, keepdims=True)
    return (x - m) / jnp.sqrt(v + eps)
def _scatter_add(tgt, idx, src, axis=0):
    return tgt.at[idx].add(src)
def _segment_sum(src, seg, n):
    return jax.ops.segment_sum(src, seg, n)

kernel_name = 'mk_conv_preact_d1_conv_nchw1024_894f9f'

def setup_inputs(seed: int = 0):
    np.random.seed(seed)
    _w = jnp.asarray
    def _rec_inputs():
        import jax
        import jax.numpy as jnp
        _gk = jax.random.key(seed)
        x = -7.109e-05 + 0.9999 * jax.random.normal(jax.random.fold_in(_gk, 1), (16, 1024, 64, 64), jnp.float32)
        return x
    x = _rec_inputs()
    def _L0_conv_setup():
        import jax, jax.numpy as jnp
        import numpy as np
        CH = 1024
        HEADS = 8
        RED = 4
        PH, PW = (16, 16)
        DPH = max(CH // RED // HEADS, 1)
        TD = DPH * HEADS
        EPS_NORM = 1e-12
        EPS_BN = 1e-05

        def _l2norm(t):
            n = jnp.sqrt(jnp.sum(t * t, axis=-1, keepdims=True))
            return t / jnp.maximum(n, EPS_NORM)
        key = jax.random.key(seed)
        ks = jax.random.split(key, 6)
        b, h, w = (16, 64, 64)
        x = jax.random.normal(ks[0], (b, CH, h, w), dtype=jnp.float32)
        w_qkv = jax.random.normal(ks[1], (3 * TD, CH), dtype=jnp.float32) * (1.0 / np.sqrt(CH))
        temperature = jnp.ones((HEADS, 1, 1), dtype=jnp.float32)
        w_proj = jax.random.normal(ks[2], (CH, TD), dtype=jnp.float32) * (1.0 / np.sqrt(TD))
        bn_gamma = jnp.ones((CH,), dtype=jnp.float32)
        bn_beta = jnp.zeros((CH,), dtype=jnp.float32)
        return {'x': x, 'w_qkv': w_qkv, 'temperature': temperature, 'w_proj': w_proj, 'bn_gamma': bn_gamma, 'bn_beta': bn_beta}
    _L0_conv_all = _L0_conv_setup()
    _L0_conv_in = {k: v for k, v in _L0_conv_all.items() if k in ('w_qkv', 'temperature', 'w_proj', 'bn_gamma', 'bn_beta', )}
    del _L0_conv_all

    return {
        "x": x,
        "L0_conv_w_qkv": _L0_conv_in["w_qkv"],
        "L0_conv_temperature": _L0_conv_in["temperature"],
        "L0_conv_w_proj": _L0_conv_in["w_proj"],
        "L0_conv_bn_gamma": _L0_conv_in["bn_gamma"],
        "L0_conv_bn_beta": _L0_conv_in["bn_beta"],
    }

def reference(x, L0_conv_w_qkv, L0_conv_temperature, L0_conv_w_proj, L0_conv_bn_gamma, L0_conv_bn_beta):
    import jax
    import jax.numpy as jnp
    def _L0_conv_ref(x, w_qkv, temperature, w_proj, bn_gamma, bn_beta):
        import jax, jax.numpy as jnp
        import numpy as np
        CH = 1024
        HEADS = 8
        RED = 4
        PH, PW = (16, 16)
        DPH = max(CH // RED // HEADS, 1)
        TD = DPH * HEADS
        EPS_NORM = 1e-12
        EPS_BN = 1e-05

        def _l2norm(t):
            n = jnp.sqrt(jnp.sum(t * t, axis=-1, keepdims=True))
            return t / jnp.maximum(n, EPS_NORM)
        b, c, h, w = x.shape
        fh, fw = (h // PH, w // PW)
        xr = x.reshape(b, c, PH, fh, PW, fw).mean(axis=(3, 5))
        qkv = jnp.einsum('ochw->ohwc', jnp.zeros((1, 1, 1, 1)))
        qkv = jnp.einsum('bchw,oc->bohw', xr, w_qkv)
        q, k, v = jnp.split(qkv, 3, axis=1)
        L = PH * PW

        def to_heads(t):
            return t.reshape(b, HEADS, DPH, L).transpose(0, 1, 3, 2)
        q, k, v = (to_heads(q), to_heads(k), to_heads(v))
        q = _l2norm(q)
        k = _l2norm(k)
        attn = jnp.einsum('bhld,bhmd->bhlm', q, k) * temperature
        attn = jax.nn.softmax(attn, axis=-1)
        out = jnp.einsum('bhlm,bhmd->bhld', attn, v)
        out = out.transpose(0, 1, 3, 2).reshape(b, TD, PH, PW)
        out = jax.image.resize(out, (b, TD, h, w), method='bilinear')
        out = jnp.einsum('bchw,oc->bohw', out, w_proj)
        mean = out.mean(axis=(0, 2, 3), keepdims=True)
        var = out.var(axis=(0, 2, 3), keepdims=True)
        out = (out - mean) * jax.lax.rsqrt(var + EPS_BN)
        out = out * bn_gamma[None, :, None, None] + bn_beta[None, :, None, None]
        return out

    def _gn(v, G=32, eps=1e-5):
        B_, C_, H_, W_ = v.shape
        g = v.reshape(B_, G, C_ // G, H_, W_)
        m = jnp.mean(g, axis=(2, 3, 4), keepdims=True)
        s = jnp.var(g, axis=(2, 3, 4), keepdims=True)
        return ((g - m) / jnp.sqrt(s + eps)).reshape(v.shape)

    def _ln_c(v, eps=1e-6):
        m = jnp.mean(v, axis=1, keepdims=True)
        s = jnp.var(v, axis=1, keepdims=True)
        return (v - m) / jnp.sqrt(s + eps)

    def _ln_t(v, eps=1e-5):
        m = jnp.mean(v, axis=-1, keepdims=True)
        s = jnp.var(v, axis=-1, keepdims=True)
        return (v - m) / jnp.sqrt(s + eps)

    def _to_tokens(v):
        B_, C_, H_, W_ = v.shape
        return v.reshape(B_, C_, H_ * W_).transpose(0, 2, 1)
    def _from_tokens(t, like):
        B_, C_, H_, W_ = like.shape
        return t.transpose(0, 2, 1).reshape(B_, C_, H_, W_)

    x = x + _L0_conv_ref(_gn(x), L0_conv_w_qkv, L0_conv_temperature, L0_conv_w_proj, L0_conv_bn_gamma, L0_conv_bn_beta)
    return x


_drawn_inputs = setup_inputs


def setup_inputs(seed=0):
    import zlib

    import numpy as np

    out = dict(_drawn_inputs(seed))
    spreads = {'L0_conv_temperature': (1.0, 0.6),
     'L0_conv_bn_gamma': (1.0, 0.2),
     'L0_conv_bn_beta': (0.0, 0.1)}
    factors = {}
    for name, (base, spread) in spreads.items():
        noise = np.random.default_rng([zlib.crc32(name.encode()), seed]).standard_normal(out[name].shape)
        drawn = base * np.exp(spread * noise) if base else spread * noise
        out[name] = jnp.asarray(drawn.astype(out[name].dtype))
    for name, factor in factors.items():
        out[name] = (out[name] * factor).astype(out[name].dtype)
    return out
```

```python
from contextlib import ExitStack

import numpy as np

import concourse.bass as bass
from concourse import mybir

F32 = mybir.dt.float32
U8 = mybir.dt.uint8
ALU = mybir.AluOpType
ACT = mybir.ActivationFunctionType
AX = mybir.AxisListType

P = 128
B, CH, H, W = 16, 1024, 64, 64
LOW = 16
POOL = H // LOW
PIX = H * W
POS = LOW * LOW
TILES = CH // P
HALF = TILES // 2
GROUP = CH // 32
HEADS, DH = 8, 32
TD = HEADS * DH
CC = TD // P
LC = POS // P
EPS_GN, EPS_BN, EPS_NORM = 1e-5, 1e-5, 1e-12
PAIRED = (0, 1, 2)
WINDOWS = (0, 5, 8)
WINDOW_OF = (0, 0, 0, 1, 1, 1, 2, 2)
SLOTS = 8
UNIT = 1024
UNITS = PIX // UNIT


def bilinear():
    src = (np.arange(H) + 0.5) / POOL - 0.5
    m = np.maximum(0.0, 1.0 - np.abs(src[:, None] - np.arange(LOW)[None, :]))
    return m / m.sum(1, keepdims=True)


def constants():
    u = bilinear()
    p = np.arange(P)
    ident = np.eye(P)
    group = (p[:, None] // GROUP == p[None, :] // GROUP) / GROUP
    gram = np.kron(u.T @ u, u.T @ u) / (B * PIX)
    gram = gram.reshape(LC, P, POS).transpose(1, 0, 2).reshape(P, LC * POS)
    rows = np.zeros((P, H))
    for r in range(H):
        rows[:, r] = u[r, WINDOWS[WINDOW_OF[r // 8]] + p // LOW]
    cols = u[:, p % LOW].T
    return np.concatenate([ident, group, gram, rows, cols], axis=1).astype(np.float32)


C_IDENT, C_GROUP, C_GRAM, C_ROWS, C_COLS, C_END = 0, 128, 256, 768, 832, 896


def program(nc, x, w_qkv, temperature, w_proj, gamma, beta, consts, out):
    x_rows = x.rearrange("b c h w -> (b c) (h w)")
    out_rows = out.rearrange("b c h w -> (b c) (h w)")

    def tile_rows(rows, b, j):
        return rows[bass.ds(b * CH + j * P, P), :]

    with ExitStack() as ctx:
        def sb(name, shape, dt=F32):
            return ctx.enter_context(nc.sbuf_tensor(name, shape, dt))

        def sem(name):
            return ctx.enter_context(nc.semaphore(name))

        slots = sb("slots", [P, SLOTS, PIX])
        late = slots[:, 4:8, :].rearrange("p s n -> p (s n)")
        w_t = late[:, 0:6144].rearrange("p (j n) -> p j n", j=TILES)
        pooled = late[:, 6144:8192].rearrange("p (h i n) -> p h i n", h=2, i=HALF)
        junk = late[:, 8192:10240].bitcast(U8).rearrange("p (k n) -> p k n", k=2)
        paired_rows = late[:, 10240:12288]
        qk_sq = late[:, 12288:13312]
        qk_n = late[:, 13312:14336].rearrange("p (l n) -> p l n", l=LC)
        v_sb = late[:, 14336:14848].rearrange("p (l n) -> p l n", l=LC)
        q_t = late[:, 14848:15360].rearrange("p (c n) -> p c n", c=CC)
        k_t = late[:, 15360:15872].rearrange("p (c n) -> p c n", c=CC)
        o_sb = late[:, 15872:16384].rearrange("p (c n) -> p c n", c=CC)
        up = sb("up", [P, H, W])
        scratch = up[:, :, :].rearrange("p a b -> p (a b)")
        e_sb = scratch[:, 0:1024].rearrange("p (h l m) -> p h l m", h=2, l=LC)
        e_t = scratch[:, 1024:2048].rearrange("p (h m l) -> p h m l", h=2, m=LC)
        a_t = scratch[:, 2048:2560].rearrange("p (l n) -> p l n", l=LC)
        a_c = scratch[:, 2560:3072].rearrange("p (l n) -> p l n", l=LC)
        g_sb = scratch[:, 3072:3584].rearrange("p (l n) -> p l n", l=LC)
        att = sb("att", [P, B, CC, POS])
        w_stage = att[:, :, :, :].rearrange("p b c n -> p (b c n)")[:, 0:6144]\
            .rearrange("p (o n) -> p o n", o=6)
        wp_t = sb("wp_t", [P, CC, CH])
        wp_n = sb("wp_n", [P, TILES, TD])
        low_t = sb("low_t", [P, 2, 3, P])
        att_now = sb("att_now", [P, CC, POS])
        con = sb("con", [P, C_END])
        ident, group = con[:, C_IDENT:C_GROUP], con[:, C_GROUP:C_GRAM]
        gram = con[:, C_GRAM:C_ROWS].rearrange("p (l n) -> p l n", l=LC)
        rows_f, cols_f = con[:, C_ROWS:C_COLS], con[:, C_COLS:C_END]
        ones = sb("ones", [P, P])
        cov_sum = sb("cov_sum", [P, CC, TD])
        cov = sb("cov", [P, CC, TD + 1])
        temp = sb("temp", [P, HEADS])
        gam, bet = sb("gam", [P, TILES]), sb("bet", [P, TILES])
        first = sb("first", [P, 2, HALF])
        sumsq = sb("sumsq", [P, 2, HALF])
        sums = sb("sums", [P, 2, HALF])
        gs = sb("gs", [P, 11, HALF])
        mean_c, dev, var_c, sq_c, v_eps, rstd, scale16, shift_c, neg_mean, minus_half, \
            per_pixel = (gs[:, i, :] for i in range(11))
        nrm = sb("nrm", [P, 2, 2 * LC * HEADS])
        norm2, rnorm = nrm[:, 0, :], nrm[:, 1, :]
        neg_max = sb("neg_max", [P, 2 * LC])
        row_sum = sb("row_sum", [P, LC, HEADS])
        row_inv = sb("row_inv", [P, LC, HEADS])
        mu = sb("mu", [P, B, CC])
        mu_d = sb("mu_d", [P, CC, B])
        mu_dt = sb("mu_dt", [B, TD])
        bn = sb("bn", [P, 6, TILES])
        bn_var, bn_mean, bn_rstd, bn_scale, bn_shift, bn_half = (bn[:, i, :] for i in range(6))
        prod = cov_sum
        ps = ctx.enter_context(nc.psum_tensor("ps", [P, 8, 512], F32))

        def bank(n, k=1):
            return ps[:, n:n + k, :].rearrange("p a b -> p (a b)")

        x_landed = [sem(f"x_landed{s}") for s in range(SLOTS)]
        stored = [sem(f"stored{s}") for s in range(SLOTS)]
        wq_landed, wp_landed, con_landed = sem("wq_landed"), sem("wp_landed"), sem("con_landed")
        set_up = sem("set_up")
        w_turned, w_copied = sem("w_turned"), sem("w_copied")
        squared, pooled_s, paired = sem("squared"), sem("pooled"), sem("paired")
        sums_ready, mean_ready, group_mean = sem("sums_ready"), sem("mean_ready"), sem("group_mean")
        dev_ready, sq_ready, group_var = sem("dev_ready"), sem("sq_ready"), sem("group_var")
        var_ready, xn_ready, qkv_done = sem("var_ready"), sem("xn_ready"), sem("qkv_done")
        qk_squared, norm_ready, norm_root = sem("qk_squared"), sem("norm_ready"), sem("norm_root")
        v_copied, qk_scaled, qk_turned = sem("v_copied"), sem("qk_scaled"), sem("qk_turned")
        qk_copied, scored, max_ready = sem("qk_copied"), sem("scored"), sem("max_ready")
        exp_done, e_turned, e_copied = sem("exp_done"), sem("e_turned"), sem("e_copied")
        mixed, o_copied, o_turned = sem("mixed"), sem("o_copied"), sem("o_turned")
        at_ready, at_mean, at_turned = sem("at_ready"), sem("at_mean"), sem("at_turned")
        att_copied, ac_ready, gram_done = sem("att_copied"), sem("ac_ready"), sem("gram_done")
        gram_copied, cov_done, cov_added = sem("gram_copied"), sem("cov_done"), sem("cov_added")
        mu_ready, mu_turned, mu_copied = sem("mu_ready"), sem("mu_turned"), sem("mu_copied")
        mu_outer, cov_ready, cov_w = sem("mu_outer"), sem("cov_ready"), sem("cov_w")
        bn_read = sem("bn_read")
        bn_var_ready, bn_rstd_ready, bn_ready = sem("bn_var_ready"), sem("bn_rstd"), sem("bn_ready")
        up_ready, att_now_ready = sem("up_ready"), sem("att_now_ready")
        low_done, low_copied = sem("low_done"), sem("low_copied")
        upsampled, scaled, added = sem("upsampled"), sem("scaled"), sem("added")

        def wait(eng, s, value):
            if not (isinstance(value, int) and value <= 0):
                eng.wait_ge(s, value)

        ATT_STEPS = (2, 3, 4, 5)

        block = ctx.enter_context(nc.Block())

        @block.sync
        def _(sp):
            def load_item(b):
                for t in range(TILES):
                    wait(sp, pooled_s, b * TILES + t - 3)
                    wait(sp, squared, b * TILES + t - 3)
                    sp.dma_start(slots[:, t % HALF, :], tile_rows(x_rows, b, t)).then_inc(x_landed[t % HALF], 16)

            load_item(0)
            with sp.Fori(1, B) as b:
                load_item(b)
            sp.wait_ge(qkv_done, 2 * B)
            sp.dma_start(slots[:, 4, :], tile_rows(x_rows, B - 1, 0)).then_inc(x_landed[4], 16)
            sp.dma_start(slots[:, 5, :], tile_rows(x_rows, B - 1, 1)).then_inc(x_landed[5], 16)
            sp.wait_ge(pooled_s, TILES * B)
            sp.wait_ge(squared, TILES * B)
            sp.dma_start(slots[:, 6, :], tile_rows(x_rows, B - 1, 2)).then_inc(x_landed[6], 16)
            sp.wait_ge(o_turned, B)
            sp.dma_start(slots[:, 7, :], tile_rows(x_rows, B - 1, 3)).then_inc(x_landed[7], 16)

            def store_item(k, b, more):
                for s in range(SLOTS):
                    sp.wait_ge(added, (k * SLOTS + s + 1) * UNITS)
                    sp.dma_start(tile_rows(out_rows, b, (s + 4) % TILES), slots[:, s, :]).then_inc(stored[s], 16)
                    if s < 2:
                        if not (isinstance(k, int) and k == 0):
                            sp.wait_ge(stored[s + 6], k * 16)
                            sp.dma_start(slots[:, s + 6, :], tile_rows(x_rows, b, (s + 10) % TILES))\
                              .then_inc(x_landed[s + 6], 16)
                    elif more:
                        sp.wait_ge(stored[s - 2], (k + 1) * 16)
                        nxt = 0 if isinstance(k, int) else b + 1
                        sp.dma_start(slots[:, s - 2, :], tile_rows(x_rows, nxt, (s + 2) % TILES))\
                          .then_inc(x_landed[s - 2], 16)

            store_item(0, B - 1, True)
            with sp.Fori(1, B - 1) as k:
                store_item(k, k - 1, True)
            store_item(B - 1, B - 2, False)
            for s in range(SLOTS):
                sp.wait_ge(stored[s], 16 * B)

        @block.gpsimd
        def _(pool):
            pool.memset(ones[:, :], 1.0 / POS).then_inc(set_up, 1)
            pool.memset(minus_half, -0.5).then_inc(set_up, 1)
            pool.memset(bn_half, -0.5).then_inc(set_up, 1)
            pool.memset(per_pixel, 1.0 / PIX).then_inc(set_up, 1)
            pool.memset(cov_sum[:, :, :], 0.0).then_inc(set_up, 1)
            pool.wait_ge(set_up, 5)

            def pair_rows(b, t):
                i = t % HALF
                if i not in PAIRED:
                    return
                pool.wait_ge(x_landed[i], (b * 2 + t // HALF + 1) * 16)
                wait(pool, pooled_s, b * TILES + t + (0 if i else -(HALF - 1 - PAIRED[-1])))
                rows = slots[:, i, :].rearrange("p (a r w) -> p a r w", r=POOL, w=W)
                pool.tensor_tensor(paired_rows.rearrange("p (a r w) -> p a r w", r=2, w=W),
                                   rows[:, :, 0:2, :], rows[:, :, 2:4, :], ALU.add)\
                    .then_inc(paired, 1)

            def group_norm(b, h):
                n = 2 * b + h
                pool.wait_ge(sums_ready, n + 1)
                pool.tensor_tensor(mean_c, sums[:, h, :], per_pixel, ALU.mult)\
                    .then_inc(mean_ready, 1)
                pool.wait_ge(squared, b * TILES + (h + 1) * HALF)
                pool.tensor_tensor(var_c, sumsq[:, h, :], per_pixel, ALU.mult)
                pool.drain()
                pool.tensor_tensor(sq_c, mean_c, first[:, h, :], ALU.subtract)
                pool.drain()
                pool.tensor_tensor(sq_c, sq_c, sq_c, ALU.mult)
                pool.drain()
                pool.tensor_tensor(var_c, var_c, sq_c, ALU.subtract)
                pool.drain()
                pool.wait_ge(dev_ready, n + 1)
                pool.tensor_tensor(sq_c, dev, dev, ALU.mult)
                pool.tensor_tensor(neg_mean, dev, mean_c, ALU.subtract)
                pool.drain()
                pool.tensor_tensor(sq_c, sq_c, var_c, ALU.add).then_inc(sq_ready, 1)
                pool.wait_ge(var_ready, n + 1)
                pool.tensor_tensor(rstd, v_eps, minus_half, ALU.pow)
                pool.drain()
                pool.tensor_scalar(scale16, rstd, 1.0 / (POOL * POOL), 0.0, ALU.mult, ALU.add)
                pool.tensor_tensor(shift_c, neg_mean, rstd, ALU.mult)
                pool.drain()
                for i in range(HALF):
                    last = pool.tensor_scalar(pooled[:, h, i, :], pooled[:, h, i, :],
                                              scale16[:, i:i + 1], shift_c[:, i:i + 1],
                                              ALU.mult, ALU.add)
                last.then_inc(xn_ready, 1)
                pool.drain()

            def item(b):
                for t in range(TILES):
                    pair_rows(b, t)
                    if t == HALF:
                        group_norm(b, 0)
                group_norm(b, 1)

            item(0)
            with pool.Fori(1, B) as b:
                item(b)

            pool.wait_ge(cov_done, B)
            pool.wait_ge(con_landed, 16)
            pool.tensor_tensor(up[:, :, :], rows_f.unsqueeze(2).to_broadcast([P, H, W]),
                               cols_f.unsqueeze(1).to_broadcast([P, H, W]), ALU.mult)\
                .then_inc(up_ready, 1)
            pool.wait_ge(att_copied, B)
            pool.tensor_copy(att_now[:, :, :], att[:, B - 1, :, :]).then_inc(att_now_ready, 1)
            pool.wait_ge(bn_var_ready, 1)
            pool.tensor_tensor(bn_rstd, bn_var, bn_half, ALU.pow).then_inc(bn_rstd_ready, 1)
            with pool.Fori(1, B) as k:
                pool.wait_ge(low_done, k * TILES)
                pool.tensor_copy(att_now[:, :, :], att[:, bass.ds(k - 1, 1), :, :].rearrange(
                    "p o c n -> p (o c) n")).then_inc(att_now_ready, 1)

        @block.scalar
        def _(act):
            act.dma_start(w_stage, w_qkv.rearrange("(o p) n -> p o n", p=P)).then_inc(wq_landed, 16)
            act.dma_start(con[:, :], consts).then_inc(con_landed, 16)
            act.dma_start(wp_n[:, :, :], w_proj.rearrange("(o p) n -> p o n", p=P))\
                .then_inc(wp_landed, 16)
            with nc.allow_non_contiguous_dma(reason="a few KiB once"):
                act.dma_start(temp[:, :], temperature.rearrange("h a b -> (a b) h")
                              .to_broadcast([P, HEADS])).then_inc(wp_landed, 16)
                act.dma_start(gam[:, :], gamma.rearrange("(o p) -> p o", p=P))\
                    .then_inc(wp_landed, 16)
                act.dma_start(bet[:, :], beta.rearrange("(o p) -> p o", p=P))\
                    .then_inc(wp_landed, 16)

            def square(b, t):
                h, i = divmod(t, HALF)
                act.wait_ge(x_landed[i], (b * 2 + h + 1) * 16)
                if i == 0:
                    wait(act, xn_ready, 2 * (b - 1) + h + 1)
                wait(act, squared, b * TILES + t - 1)
                act.activation(junk[:, t % 2, :], slots[:, i, :], ACT.Square, bias=slots[:, i, 0:1],
                               scale=-1.0, accum_out=sumsq[:, h, i:i + 1]).then_inc(squared, 1)

            def item(b, a, tiles):
                for t in range(TILES):
                    if a is not None and t == 1:
                        act.wait_ge(norm_ready, a + 1)
                        act.activation(rnorm, norm2, ACT.Sqrt).then_inc(norm_root, 1)
                    if a is not None and t in ATT_STEPS:
                        n = a * 4 + t - 2
                        act.wait_ge(max_ready, n + 1)
                        if t > ATT_STEPS[0]:
                            act.wait_ge(e_turned, n)
                        for u in range(2):
                            for lc in range(LC):
                                last = act.activation(
                                    e_sb[:, u, lc, :], bank(3 + u)[:, lc * POS:(lc + 1) * POS],
                                    ACT.Exp, bias=neg_max[:, u * LC + lc:u * LC + lc + 1],
                                    accum_out=row_sum[:, lc, 2 * (t - 2) + u:2 * (t - 2) + u + 1])
                        last.then_inc(exp_done, 1)
                    if tiles:
                        square(b, t)
                    if a is not None and t == 0:
                        act.wait_ge(qkv_done, 2 * a + 2)
                        act.activation(qk_sq, bank(0, 2), ACT.Square).then_inc(qk_squared, 1)
                    if a is not None and t == 1:
                        act.wait_ge(qk_turned, a + 1)
                        act.activation(q_t, bank(5), ACT.Copy)
                        act.activation(k_t, bank(6), ACT.Copy).then_inc(qk_copied, 1)
                if a is not None:
                    act.wait_ge(at_turned, a + 1)
                    for cc in range(CC):
                        dst = att[:, bass.ds(a, 1), cc, :].rearrange("p o n -> p (o n)")
                        m = mu[:, bass.ds(a, 1), cc]
                        last = act.activation(dst, bank(6)[:, cc * POS:(cc + 1) * POS], ACT.Copy,
                                              accum_out=m)
                    last.then_inc(att_copied, 1)
                    act.wait_ge(gram_done, a + 1)
                    act.activation(g_sb, bank(4), ACT.Copy).then_inc(gram_copied, 1)

            item(0, None, True)
            with act.Fori(1, B) as b:
                item(b, b - 1, True)
            item(None, B - 1, False)

            def low_copy(n, i, waits=True):
                act.wait_ge(low_done, n + 1)
                wait(act, upsampled, (n - 1) * UNITS)
                act.activation(low_t[:, i, :, :], bank(6)[:, 0:3 * P]
                               .rearrange("p (w n) -> p w n", w=3), ACT.Copy)\
                    .then_inc(low_copied, 1)

            def scale_item(k, last_item):
                for s in range(SLOTS):
                    n = k * SLOTS + s
                    if not (last_item and s == SLOTS - 1):
                        low_copy(n + 1, (s + 1) % 2)
                    o = (s + 4) % TILES
                    for u in range(UNITS):
                        act.wait_ge(upsampled, n * UNITS + u + 1)
                        act.activation(bank(2 * u, 2), bank(2 * u, 2), ACT.Identity,
                                       bias=bn_shift[:, o:o + 1], scale=bn_scale[:, o:o + 1])\
                            .then_inc(scaled, 1)

            low_copy(0, 0)
            act.wait_ge(bn_ready, 1)
            scale_item(0, False)
            with act.Fori(1, B - 1) as k:
                scale_item(k, False)
            scale_item(B - 1, True)

        @block.vector
        def _(dve):
            for n in range(TILES):
                dve.wait_ge(w_turned, n + 1)
                dve.tensor_copy(w_t[:, n, :], bank(2 * (n % 2), 2)[:, 0:768]).then_inc(w_copied, 1)
            for n in range(2 * CC):
                dve.wait_ge(w_turned, TILES + n + 1)
                cc, g = divmod(n, 2)
                dve.tensor_copy(wp_t[:, cc, g * 512:(g + 1) * 512], bank(4 + n % 2))\
                    .then_inc(w_copied, 1)

            def pool_tile(b, t):
                h, i = divmod(t, HALF)
                if i == 0:
                    wait(dve, qkv_done, 2 * (b - 1) + h + 1)
                dst = pooled[:, h, i, :].rearrange("p (a b) -> p a b", a=LOW)
                dve.wait_ge(x_landed[i], (2 * b + h + 1) * 16)
                dve.tensor_copy(first[:, h, i:i + 1], slots[:, i, 0:1])
                if i in PAIRED:
                    dve.wait_ge(paired, b * 2 * len(PAIRED) + h * len(PAIRED) + PAIRED.index(i) + 1)
                    src = paired_rows.rearrange("p (a r b c) -> p a b r c", a=LOW, r=2, b=LOW)
                else:
                    src = slots[:, i, :].rearrange("p (a r b c) -> p a b r c", a=LOW, r=POOL, b=LOW)
                dve.tensor_reduce(dst, src, AX.XY, ALU.add).then_inc(pooled_s, 1)

            def half_sums(b, h):
                dve.wait_ge(pooled_s, b * TILES + (h + 1) * HALF)
                dve.tensor_reduce(sums[:, h, :], pooled[:, h, :, :], AX.X, ALU.add)\
                    .then_inc(sums_ready, 1)

            def half_dev(b, h):
                dve.wait_ge(group_mean, 2 * b + h + 1)
                dve.tensor_tensor(dev, mean_c, bank(7)[:, 256:256 + HALF], ALU.subtract)\
                    .then_inc(dev_ready, 1)

            def half_var(b, h):
                dve.wait_ge(group_var, 2 * b + h + 1)
                dve.tensor_scalar(v_eps, bank(7)[:, 256:256 + HALF], 1.0, EPS_GN, ALU.mult, ALU.add)\
                    .then_inc(var_ready, 1)

            def item(b, a, tiles):
                at = a is not None
                for t in range(TILES):
                    if at and t == 1:
                        dve.wait_ge(norm_root, a + 1)
                        dve.reciprocal(rnorm, rnorm)
                        dve.drain()
                        r4 = rnorm.rearrange("p (l s h) -> p l s h", l=LC, s=2)
                        for lc in range(LC):
                            dve.tensor_tensor(r4[:, lc, 1, :], r4[:, lc, 1, :], temp[:, :], ALU.mult)
                        dve.drain()
                        dve.tensor_tensor(
                            late[:, 13312:14336].rearrange("p (g d) -> p g d", d=DH),
                            bank(0, 2).rearrange("p (g d) -> p g d", d=DH),
                            rnorm.unsqueeze(2).to_broadcast([P, 2 * LC * HEADS, DH]), ALU.mult)\
                            .then_inc(qk_scaled, 1)
                    if at and t in ATT_STEPS:
                        n = a * 4 + t - 2
                        dve.wait_ge(scored, n + 1)
                        if t > ATT_STEPS[0]:
                            dve.wait_ge(exp_done, n)
                        dve.tensor_reduce(neg_max[:, :], bank(3, 2).rearrange(
                            "p (g m) -> p g m", m=POS), AX.X, ALU.max, negate=True)\
                            .then_inc(max_ready, 1)
                    if tiles and t == HALF:
                        half_dev(b, 0)
                    if at and t == 7:
                        dve.wait_ge(o_turned, a + 1)
                        dve.tensor_tensor(
                            scratch[:, 2048:2560].rearrange("p (g d) -> p g d", d=DH),
                            bank(5).rearrange("p (g d) -> p g d", d=DH),
                            row_inv[:, :, :].rearrange("p l h -> p (l h)").unsqueeze(2)
                            .to_broadcast([P, LC * HEADS, DH]), ALU.mult).then_inc(at_ready, 1)
                    if tiles:
                        pool_tile(b, t)
                    if tiles and t == HALF:
                        half_var(b, 0)
                    if at and t == 0:
                        dve.wait_ge(qkv_done, 2 * a + 2)
                        dve.tensor_copy(v_sb, bank(2).rearrange("p (l n) -> p l n", l=LC))\
                            .then_inc(v_copied, 1)
                        dve.wait_ge(qk_squared, a + 1)
                        dve.tensor_reduce(norm2, qk_sq.rearrange("p (g d) -> p g d", d=DH), AX.X,
                                          ALU.add)
                        dve.drain()
                        dve.tensor_scalar(norm2, norm2, EPS_NORM ** 2, None, ALU.max)\
                            .then_inc(norm_ready, 1)
                    if at and t in ATT_STEPS:
                        n = a * 4 + t - 2
                        dve.wait_ge(e_turned, n + 1)
                        dve.tensor_copy(scratch[:, 1024:2048], bank(5, 2)).then_inc(e_copied, 1)
                    if at and t == 6:
                        dve.wait_ge(mixed, a * 4 + 4)
                        dve.tensor_copy(o_sb, bank(7).rearrange("p (c n) -> p c n", c=CC))\
                            .then_inc(o_copied, 1)
                        dve.wait_ge(exp_done, a * 4 + 4)
                        dve.reciprocal(row_inv[:, :, :], row_sum[:, :, :])
                        dve.drain()
                    if tiles and t == HALF - 1:
                        half_sums(b, 0)
                if tiles:
                    half_sums(b, 1)
                if at:
                    dve.wait_ge(at_mean, a + 1)
                    dve.tensor_tensor(a_c, a_t, bank(3)[:, 0:TD].unsqueeze(1)
                                      .to_broadcast([P, LC, TD]), ALU.subtract)\
                        .then_inc(ac_ready, 1)
                if tiles:
                    half_dev(b, 1)
                    half_var(b, 1)
                if at:
                    dve.wait_ge(cov_done, a + 1)
                    dve.tensor_tensor(cov_sum[:, :, :], cov_sum[:, :, :], bank(3).rearrange(
                        "p (c n) -> p c n", c=CC), ALU.add).then_inc(cov_added, 1)

            dve.wait_ge(set_up, 5)
            dve.wait_ge(wp_landed, 64)
            item(0, None, True)
            with dve.Fori(1, B) as b:
                item(b, b - 1, True)
            item(None, B - 1, False)

            dve.wait_ge(att_copied, B)
            for cc in range(CC):
                dve.tensor_reduce(cov[:, cc, TD:TD + 1], mu[:, :, cc], AX.X, ALU.add)
            dve.drain()
            for cc in range(CC):
                dve.tensor_scalar(cov[:, cc, TD:TD + 1], cov[:, cc, TD:TD + 1], 1.0 / (B * POS),
                                  None, ALU.mult)
                dve.tensor_scalar(mu_d[:, cc, :], mu[:, :, cc], 1.0 / POS, None, ALU.mult)
            dve.drain()
            for cc in range(CC):
                last = dve.tensor_scalar(mu_d[:, cc, :], mu_d[:, cc, :], cov[:, cc, TD:TD + 1],
                                         1.0 / float(np.sqrt(B)), ALU.subtract, ALU.mult)
            last.then_inc(mu_ready, 1)
            dve.wait_ge(mu_turned, 1)
            dve.tensor_copy(mu_dt[:, :], bank(0)[0:B, 0:TD]).then_inc(mu_copied, 1)
            dve.wait_ge(mu_outer, 1)
            dve.wait_ge(cov_added, B)
            dve.tensor_tensor(cov[:, :, 0:TD], cov_sum[:, :, :], bank(1).rearrange(
                "p (c n) -> p c n", c=CC), ALU.add).then_inc(cov_ready, 1)
            for o in range(TILES):
                dve.wait_ge(cov_w, o + 1)
                wait(dve, bn_read, o - 1)
                dve.tensor_copy(bn_mean[:, o:o + 1], bank(2 + o % 4)[:, TD:TD + 1])
                last = dve.tensor_tensor_reduce(
                    out=prod[:, o % 2, :], in0=bank(2 + o % 4)[:, 0:TD], in1=wp_n[:, o, :], scale=1.0,
                    scalar=0.0, op0=ALU.mult, op1=ALU.add, accum_out=bn_var[:, o:o + 1])
                last.then_inc(bn_read, 1)
            dve.wait_ge(bn_read, TILES)
            dve.tensor_scalar(bn_var, bn_var, 0.0, EPS_BN, ALU.max, ALU.add)\
                .then_inc(bn_var_ready, 1)
            dve.wait_ge(bn_rstd_ready, 1)
            dve.tensor_tensor(bn_scale, bn_rstd, gam[:, :], ALU.mult)
            dve.drain()
            dve.tensor_tensor(bn_mean, bn_mean, bn_scale, ALU.mult)
            dve.drain()
            dve.tensor_tensor(bn_shift, bet[:, :], bn_mean, ALU.subtract).then_inc(bn_ready, 1)

            def add_item(k):
                for s in range(SLOTS):
                    if s < HALF:
                        dve.wait_ge(x_landed[s], (k + 2 * B) * 16)
                    else:
                        dve.wait_ge(x_landed[s], (k + 1) * 16)
                    for u in range(UNITS):
                        dve.wait_ge(scaled, (k * SLOTS + s) * UNITS + u + 1)
                        part = slots[:, s, u * UNIT:(u + 1) * UNIT]
                        dve.tensor_tensor(part, part, bank(2 * u, 2), ALU.add).then_inc(added, 1)

            add_item(0)
            with dve.Fori(1, B) as k:
                add_item(k)

        @block.tensor
        def _(pe):
            pe.wait_ge(con_landed, 16)
            pe.wait_ge(wq_landed, 16)
            for j in range(TILES):
                if j >= 2:
                    pe.wait_ge(w_copied, j - 1)
                for o in range(6):
                    last = pe.transpose(bank(2 * (j % 2), 2)[:, o * P:(o + 1) * P],
                                        w_stage[:, o, j * P:(j + 1) * P], ident)
                last.then_inc(w_turned, 1)
            pe.wait_ge(wp_landed, 64)
            for n in range(2 * CC):
                if n >= 2:
                    pe.wait_ge(w_copied, TILES + n - 1)
                cc, g = divmod(n, 2)
                for o in range(4):
                    last = pe.transpose(bank(4 + n % 2)[:, o * P:(o + 1) * P],
                                        wp_n[:, 4 * g + o, cc * P:(cc + 1) * P], ident)
                last.then_inc(w_turned, 1)
            pe.wait_ge(set_up, 5)
            pe.wait_ge(w_copied, TILES + 2 * CC)

            def group_means(b, h):
                pe.wait_ge(mean_ready, 2 * b + h + 1)
                pe.matmul(bank(7)[:, 256:256 + HALF], lhsT=group, rhs=mean_c, start=True,
                          stop=True, skip_group_check=True).then_inc(group_mean, 1)

            def group_vars(b, h):
                pe.wait_ge(sq_ready, 2 * b + h + 1)
                pe.matmul(bank(7)[:, 256:256 + HALF], lhsT=group, rhs=sq_c, start=True,
                          stop=True, skip_group_check=True).then_inc(group_var, 1)

            def qkv(b, h):
                pe.wait_ge(xn_ready, 2 * b + h + 1)
                if h == 0:
                    wait(pe, qk_scaled, b)
                    wait(pe, v_copied, b)
                for i in range(HALF):
                    j = h * HALF + i
                    for lc in range(LC):
                        lhs = pooled[:, h, i, lc * P:(lc + 1) * P]
                        pe.matmul(bank(lc), lhsT=lhs, rhs=w_t[:, j, 0:2 * TD], start=(j == 0),
                                  stop=(j == TILES - 1), skip_group_check=True)
                        last = pe.matmul(bank(2)[:, lc * TD:(lc + 1) * TD], lhsT=lhs,
                                         rhs=w_t[:, j, 2 * TD:3 * TD], start=(j == 0 and lc == 0),
                                         stop=(j == TILES - 1), skip_group_check=True)
                last.then_inc(qkv_done, 1)

            def scores(a, step):
                n = a * 4 + step - 2
                if step == ATT_STEPS[0]:
                    pe.wait_ge(qk_copied, a + 1)
                else:
                    pe.wait_ge(exp_done, n)
                for u in range(2):
                    hd = 2 * (step - 2) + u
                    cc, r = divmod(hd * DH, P)
                    for lc in range(LC):
                        last = pe.matmul(bank(3 + u)[:, lc * POS:(lc + 1) * POS],
                                         lhsT=q_t[r:r + DH, cc, lc * P:(lc + 1) * P],
                                         rhs=k_t[r:r + DH, cc, :], start=True, stop=True,
                                         skip_group_check=True)
                last.then_inc(scored, 1)

            def turn_e(a, step):
                n = a * 4 + step - 2
                pe.wait_ge(exp_done, n + 1)
                if step > ATT_STEPS[0]:
                    pe.wait_ge(e_copied, n)
                for u in range(2):
                    for lc in range(LC):
                        for mc in range(LC):
                            last = pe.transpose(
                                bank(5 + u)[:, mc * POS + lc * P:mc * POS + (lc + 1) * P],
                                e_sb[:, u, lc, mc * P:(mc + 1) * P], ident)
                last.then_inc(e_turned, 1)

            def mix(a, step):
                n = a * 4 + step - 2
                pe.wait_ge(e_copied, n + 1)
                for u in range(2):
                    hd = 2 * (step - 2) + u
                    cc, r = divmod(hd * DH, P)
                    for mc in range(LC):
                        last = pe.matmul(bank(7)[r:r + DH, cc * POS:(cc + 1) * POS],
                                         lhsT=v_sb[:, mc, hd * DH:(hd + 1) * DH],
                                         rhs=e_t[:, u, mc, :], start=(mc == 0),
                                         stop=(mc == LC - 1), skip_group_check=True)
                last.then_inc(mixed, 1)

            def item(b, a, tiles):
                at = a is not None
                for t in range(TILES):
                    if tiles and t == HALF:
                        group_vars(b, 0)
                        if not at:
                            qkv(b, 0)
                    if at and t == 1:
                        pe.wait_ge(qk_scaled, a + 1)
                        for s in range(2):
                            for cc in range(CC):
                                for lc in range(LC):
                                    last = pe.transpose(
                                        bank(5 + s)[:, cc * POS + lc * P:cc * POS + (lc + 1) * P],
                                        qk_n[:, lc, s * TD + cc * P:s * TD + (cc + 1) * P], ident)
                        last.then_inc(qk_turned, 1)
                        scores(a, 2)
                    if at and t in ATT_STEPS:
                        turn_e(a, t)
                        if t < ATT_STEPS[-1]:
                            scores(a, t + 1)
                        if t == HALF and tiles:
                            qkv(b, 0)
                        mix(a, t)
                    if at and t == 6:
                        pe.wait_ge(o_copied, a + 1)
                        for lc in range(LC):
                            for cc in range(CC):
                                last = pe.transpose(
                                    bank(5)[:, lc * TD + cc * P:lc * TD + (cc + 1) * P],
                                    o_sb[:, cc, lc * P:(lc + 1) * P], ident)
                        last.then_inc(o_turned, 1)
                    if at and t == 7:
                        pe.wait_ge(at_ready, a + 1)
                        for lc in range(LC):
                            last = pe.matmul(bank(3)[:, 0:TD], lhsT=ones[:, :], rhs=a_t[:, lc, :],
                                             start=(lc == 0), stop=(lc == LC - 1))
                        last.then_inc(at_mean, 1)
                        for cc in range(CC):
                            for lc in range(LC):
                                last = pe.transpose(
                                    bank(6)[:, cc * POS + lc * P:cc * POS + (lc + 1) * P],
                                    a_t[:, lc, cc * P:(cc + 1) * P], ident)
                        last.then_inc(at_turned, 1)
                    if tiles and t == HALF - 1:
                        group_means(b, 0)
                if at:
                    pe.wait_ge(ac_ready, a + 1)
                    for lo in range(LC):
                        for lc in range(LC):
                            last = pe.matmul(bank(4)[:, lo * TD:(lo + 1) * TD],
                                             lhsT=gram[:, lc, lo * P:(lo + 1) * P],
                                             rhs=a_c[:, lc, :], start=(lc == 0),
                                             stop=(lc == LC - 1), skip_group_check=True)
                    last.then_inc(gram_done, 1)
                if tiles:
                    group_means(b, 1)
                    group_vars(b, 1)
                if at:
                    pe.wait_ge(gram_copied, a + 1)
                    for cc in range(CC):
                        for lc in range(LC):
                            last = pe.matmul(bank(3)[:, cc * TD:(cc + 1) * TD],
                                             lhsT=a_c[:, lc, cc * P:(cc + 1) * P],
                                             rhs=g_sb[:, lc, :], start=(lc == 0),
                                             stop=(lc == LC - 1), skip_group_check=True)
                    last.then_inc(cov_done, 1)
                if tiles:
                    qkv(b, 1)

            item(0, None, True)
            with pe.Fori(1, B) as b:
                item(b, b - 1, True)
            item(None, B - 1, False)

            pe.wait_ge(mu_ready, 1)
            for cc in range(CC):
                last = pe.transpose(bank(0)[0:B, cc * P:(cc + 1) * P], mu_d[:, cc, :], ident)
            last.then_inc(mu_turned, 1)
            pe.wait_ge(mu_copied, 1)
            for cc in range(CC):
                last = pe.matmul(bank(1)[:, cc * TD:(cc + 1) * TD],
                                 lhsT=mu_dt[:, cc * P:(cc + 1) * P], rhs=mu_dt[:, :], start=True,
                                 stop=True, skip_group_check=True)
            last.then_inc(mu_outer, 1)
            pe.wait_ge(cov_ready, 1)
            for o in range(TILES):
                if o >= 4:
                    pe.wait_ge(bn_read, o - 3)
                for cc in range(CC):
                    last = pe.matmul(bank(2 + o % 4)[:, 0:TD + 1],
                                     lhsT=wp_t[:, cc, o * P:(o + 1) * P], rhs=cov[:, cc, :],
                                     start=(cc == 0), stop=(cc == CC - 1))
                last.then_inc(cov_w, 1)

            def project(n, s, fresh):
                o = (s + 4) % TILES
                if fresh is not None:
                    pe.wait_ge(att_now_ready, fresh)
                wait(pe, added, (n - 1) * UNITS)
                wait(pe, low_copied, n)
                for w, row in enumerate(WINDOWS):
                    for cc in range(CC):
                        last = pe.matmul(bank(6)[:, w * P:(w + 1) * P],
                                         lhsT=att_now[:, cc, row * LOW:row * LOW + P],
                                         rhs=wp_t[:, cc, o * P:(o + 1) * P], start=(cc == 0),
                                         stop=(cc == CC - 1), skip_group_check=True)
                last.then_inc(low_done, 1)

            def upsample_item(k, last_item):
                for s in range(SLOTS):
                    n = k * SLOTS + s
                    if s < SLOTS - 1:
                        project(n + 1, s + 1, None)
                    elif not last_item:
                        project(n + 1, 0, k + 2)
                    pe.wait_ge(low_copied, n + 1)
                    for u in range(UNITS):
                        wait(pe, added, (n - 1) * UNITS + u + 1)
                        if u == 3 and not (last_item and s == SLOTS - 1):
                            pe.wait_ge(low_copied, n + 2)
                        for v in range(2):
                            blk = 2 * u + v
                            last = pe.matmul(bank(blk), lhsT=low_t[:, s % 2, WINDOW_OF[blk], :],
                                             rhs=up[:, blk * 8:(blk + 1) * 8, :], start=True,
                                             stop=True)
                        last.then_inc(upsampled, 1)

            pe.wait_ge(bn_read, TILES)
            project(0, 0, 1)
            pe.wait_ge(up_ready, 1)
            upsample_item(0, False)
            with pe.Fori(1, B - 1) as k:
                upsample_item(k, False)
            upsample_item(B - 1, True)


_INS = ["x", "L0_conv_w_qkv", "L0_conv_temperature", "L0_conv_w_proj", "L0_conv_bn_gamma",
        "L0_conv_bn_beta"]


def kernel(**inputs):
    import concourse.bacc as bacc
    from concourse.bass_utils import run_bass_kernel_spmd

    nc = bacc.Bacc("TRN2", target_bir_lowering=False, num_devices=1)
    arrays, args = {}, []
    for name in _INS:
        a = np.ascontiguousarray(inputs[name])
        arrays[f"in_{name}"] = a
        args.append(nc.dram_tensor(f"in_{name}", a.shape, mybir.dt.from_np(a.dtype),
                                   kind="ExternalInput").ap())
    table = constants()
    arrays["tables"] = table
    tab = nc.dram_tensor("tables", table.shape, F32, kind="ExternalInput").ap()
    out = nc.dram_tensor("out", (B, CH, H, W), F32, kind="ExternalOutput").ap()
    program(nc, *args, tab, out)
    r = run_bass_kernel_spmd(nc, [arrays], core_ids=[0])
    return r.results[0]["out"]
```

```python
from contextlib import ExitStack

import numpy as np

import concourse.bass as bass
from concourse import mybir

F32 = mybir.dt.float32
U8 = mybir.dt.uint8
ALU = mybir.AluOpType
ACT = mybir.ActivationFunctionType
AX = mybir.AxisListType

P = 128
B, CH, H, W = 16, 1024, 64, 64
LOW = 16
POOL = H // LOW
PIX = H * W
POS = LOW * LOW
TILES = CH // P
HALF = TILES // 2
GROUP = CH // 32
HEADS, DH = 8, 32
TD = HEADS * DH
CC = TD // P
LC = POS // P
EPS_GN, EPS_BN, EPS_NORM = 1e-5, 1e-5, 1e-12
PAIRED = (0, 2, 3, 4, 6)
PAIR_HEADS = 2
ROUNDS = HEADS // PAIR_HEADS
WINDOWS = (0, 5, 8)
WINDOW_OF = (0, 0, 0, 1, 1, 1, 2, 2)
SLOTS = 8
UNIT = 1024
UNITS = PIX // UNIT


def bilinear():
    src = (np.arange(H) + 0.5) / POOL - 0.5
    m = np.maximum(0.0, 1.0 - np.abs(src[:, None] - np.arange(LOW)[None, :]))
    return m / m.sum(1, keepdims=True)


def constants():
    u = bilinear()
    p = np.arange(P)
    ident = np.eye(P)
    group = (p[:, None] // GROUP == p[None, :] // GROUP) / GROUP
    gram = np.kron(u.T @ u, u.T @ u) / (B * PIX)
    gram = gram.reshape(LC, P, POS).transpose(1, 0, 2).reshape(P, LC * POS)
    rows = np.zeros((P, H))
    for r in range(H):
        rows[:, r] = u[r, WINDOWS[WINDOW_OF[r // 8]] + p // LOW]
    cols = u[:, p % LOW].T
    return np.concatenate([ident, group, gram, rows, cols], axis=1).astype(np.float32)


C_IDENT, C_GROUP, C_GRAM, C_ROWS, C_COLS, C_END = 0, 128, 256, 768, 832, 896


def program(nc, x, w_qkv, temperature, w_proj, gamma, beta, consts, out):
    x_rows = x.rearrange("b c h w -> (b c) (h w)")
    out_rows = out.rearrange("b c h w -> (b c) (h w)")

    def tile_rows(rows, b, j):
        return rows[bass.ds(b * CH + j * P, P), :]

    with ExitStack() as ctx:
        def sb(name, shape, dt=F32):
            return ctx.enter_context(nc.sbuf_tensor(name, shape, dt))

        def sem(name):
            return ctx.enter_context(nc.semaphore(name))

        slots = sb("slots", [P, SLOTS, PIX])
        late = slots[:, 4:8, :].rearrange("p s n -> p (s n)")
        w_t = late[:, 0:6144].rearrange("p (j n) -> p j n", j=TILES)
        pooled = late[:, 6144:8192].rearrange("p (h i n) -> p h i n", h=2, i=HALF)
        junk = late[:, 8192:10240].bitcast(U8).rearrange("p (k n) -> p k n", k=2)
        paired_rows = late[:, 10240:12288]
        q_m = late[:, 12288:14336].rearrange("p (c g n) -> p c g n", c=CC, g=P // DH)
        k_t = late[:, 14336:14848].rearrange("p (c n) -> p c n", c=CC)
        v_sb = late[:, 14848:15360].rearrange("p (l n) -> p l n", l=LC)
        o_sb = late[:, 15360:15872].rearrange("p (c n) -> p c n", c=CC)
        up = sb("up", [P, H, W])
        scratch = up[:, :, :].rearrange("p a b -> p (a b)")
        e_sb = scratch[:, 0:1024].rearrange("p (h l m) -> p h l m", h=2, l=LC)
        e_t = scratch[:, 1024:2048].rearrange("p (h m l) -> p h m l", h=2, m=LC)
        qk_sq = scratch[:, 0:1024]
        qk_n = scratch[:, 1024:2048].rearrange("p (l n) -> p l n", l=LC)
        a_t = scratch[:, 2048:2560].rearrange("p (l n) -> p l n", l=LC)
        a_c = scratch[:, 2560:3072].rearrange("p (l n) -> p l n", l=LC)
        g_sb = scratch[:, 3072:3584].rearrange("p (l n) -> p l n", l=LC)
        att = sb("att", [P, B, CC, POS])
        w_stage = att[:, :, :, :].rearrange("p b c n -> p (b c n)")[:, 0:6144]\
            .rearrange("p (o n) -> p o n", o=6)
        wp_t = sb("wp_t", [P, CC, CH])
        wp_n = sb("wp_n", [P, TILES, TD])
        low_t = sb("low_t", [P, 2, 3, P])
        att_now = sb("att_now", [P, CC, POS])
        con = sb("con", [P, C_END])
        ident, group = con[:, C_IDENT:C_GROUP], con[:, C_GROUP:C_GRAM]
        gram = con[:, C_GRAM:C_ROWS].rearrange("p (l n) -> p l n", l=LC)
        rows_f, cols_f = con[:, C_ROWS:C_COLS], con[:, C_COLS:C_END]
        ones = sb("ones", [P, P])
        cov_sum = sb("cov_sum", [P, CC, TD])
        cov = sb("cov", [P, CC, TD + 1])
        temp = sb("temp", [P, HEADS])
        gam, bet = sb("gam", [P, TILES]), sb("bet", [P, TILES])
        first = sb("first", [P, 2, HALF])
        sumsq = sb("sumsq", [P, 2, HALF])
        sums = sb("sums", [P, 2, HALF])
        gs = sb("gs", [P, 11, HALF])
        mean_c, dev, var_c, sq_c, v_eps, rstd, scale16, shift_c, neg_mean, minus_half, \
            per_pixel = (gs[:, i, :] for i in range(11))
        nrm = sb("nrm", [P, 2, 2 * LC * HEADS])
        norm2, rnorm = nrm[:, 0, :], nrm[:, 1, :]
        neg_max = sb("neg_max", [P, 2 * LC])
        row_sum = sb("row_sum", [P, LC, HEADS])
        row_inv = sb("row_inv", [P, LC, HEADS])
        mu = sb("mu", [P, B, CC])
        mu_d = sb("mu_d", [P, CC, B])
        mu_dt = sb("mu_dt", [B, TD])
        bn = sb("bn", [P, 6, TILES])
        bn_var, bn_mean, bn_rstd, bn_scale, bn_shift, bn_half = (bn[:, i, :] for i in range(6))
        prod = cov_sum
        ps = ctx.enter_context(nc.psum_tensor("ps", [P, 8, 512], F32))

        def bank(n, k=1):
            return ps[:, n:n + k, :].rearrange("p a b -> p (a b)")

        x_landed = [sem(f"x_landed{s}") for s in range(SLOTS)]
        stored = [sem(f"stored{s}") for s in range(SLOTS)]
        wq_landed, wp_landed, con_landed = sem("wq_landed"), sem("wp_landed"), sem("con_landed")
        set_up = sem("set_up")
        w_turned, w_copied = sem("w_turned"), sem("w_copied")
        squared, pooled_s, paired = sem("squared"), sem("pooled"), sem("paired")
        sums_ready, mean_ready, group_mean = sem("sums_ready"), sem("mean_ready"), sem("group_mean")
        dev_ready, sq_ready, group_var = sem("dev_ready"), sem("sq_ready"), sem("group_var")
        var_ready, xn_ready, qkv_part = sem("var_ready"), sem("xn_ready"), sem("qkv_part")
        qk_squared, norm_ready, norm_root = sem("qk_squared"), sem("norm_ready"), sem("norm_root")
        qk_scaled, qk_turned = sem("qk_scaled"), sem("qk_turned")
        qk_copied, scored, max_ready = sem("qk_copied"), sem("scored"), sem("max_ready")
        exp_done, e_turned, e_copied = sem("exp_done"), sem("e_turned"), sem("e_copied")
        mixed, o_copied, o_turned = sem("mixed"), sem("o_copied"), sem("o_turned")
        at_ready, at_mean, at_turned = sem("at_ready"), sem("at_mean"), sem("at_turned")
        att_copied, ac_ready, gram_done = sem("att_copied"), sem("ac_ready"), sem("gram_done")
        gram_copied, cov_done, cov_added = sem("gram_copied"), sem("cov_done"), sem("cov_added")
        mu_ready, mu_turned, mu_copied = sem("mu_ready"), sem("mu_turned"), sem("mu_copied")
        mu_outer, cov_ready, cov_w = sem("mu_outer"), sem("cov_ready"), sem("cov_w")
        bn_read = sem("bn_read")
        bn_var_ready, bn_rstd_ready, bn_ready = sem("bn_var_ready"), sem("bn_rstd"), sem("bn_ready")
        up_ready, att_now_ready = sem("up_ready"), sem("att_now_ready")
        low_done, low_copied = sem("low_done"), sem("low_copied")
        upsampled, scaled, added = sem("upsampled"), sem("scaled"), sem("added")

        def wait(eng, s, value):
            if not (isinstance(value, int) and value <= 0):
                eng.wait_ge(s, value)

        ROUND_STEP = (5, 6, 7, 0)

        def bodies(eng, body):
            body(0, True, False, False)
            body(1, True, True, False)
            with eng.Fori(2, B) as b:
                body(b, True, True, True)
            body(B, False, True, True)
            body(B + 1, False, False, True)

        block = ctx.enter_context(nc.Block())

        @block.sync
        def _(sp):
            def load_item(b):
                for t in range(TILES):
                    wait(sp, pooled_s, b * TILES + t - 3)
                    wait(sp, squared, b * TILES + t - 3)
                    sp.dma_start(slots[:, t % HALF, :], tile_rows(x_rows, b, t)).then_inc(x_landed[t % HALF], 16)

            load_item(0)
            with sp.Fori(1, B) as b:
                load_item(b)
            sp.wait_ge(qkv_part, TILES * B)
            sp.dma_start(slots[:, 4, :], tile_rows(x_rows, B - 1, 0)).then_inc(x_landed[4], 16)
            sp.dma_start(slots[:, 5, :], tile_rows(x_rows, B - 1, 1)).then_inc(x_landed[5], 16)
            sp.wait_ge(pooled_s, TILES * B)
            sp.wait_ge(squared, TILES * B)
            sp.dma_start(slots[:, 6, :], tile_rows(x_rows, B - 1, 2)).then_inc(x_landed[6], 16)
            sp.wait_ge(o_turned, B)
            sp.dma_start(slots[:, 7, :], tile_rows(x_rows, B - 1, 3)).then_inc(x_landed[7], 16)

            def store_item(k, b, more):
                for s in range(SLOTS):
                    sp.wait_ge(added, (k * SLOTS + s + 1) * UNITS)
                    sp.dma_start(tile_rows(out_rows, b, (s + 4) % TILES), slots[:, s, :]).then_inc(stored[s], 16)
                    if s < 2:
                        if not (isinstance(k, int) and k == 0):
                            sp.wait_ge(stored[s + 6], k * 16)
                            sp.dma_start(slots[:, s + 6, :], tile_rows(x_rows, b, (s + 10) % TILES))\
                              .then_inc(x_landed[s + 6], 16)
                    elif more:
                        sp.wait_ge(stored[s - 2], (k + 1) * 16)
                        nxt = 0 if isinstance(k, int) else b + 1
                        sp.dma_start(slots[:, s - 2, :], tile_rows(x_rows, nxt, (s + 2) % TILES))\
                          .then_inc(x_landed[s - 2], 16)

            store_item(0, B - 1, True)
            with sp.Fori(1, B - 1) as k:
                store_item(k, k - 1, True)
            store_item(B - 1, B - 2, False)
            for s in range(SLOTS):
                sp.wait_ge(stored[s], 16 * B)

        @block.gpsimd
        def _(pool):
            pool.memset(q_m, 0.0).then_inc(set_up, 1)
            pool.memset(ones[:, :], 1.0 / POS).then_inc(set_up, 1)
            pool.memset(minus_half, -0.5).then_inc(set_up, 1)
            pool.memset(bn_half, -0.5).then_inc(set_up, 1)
            pool.memset(per_pixel, 1.0 / PIX).then_inc(set_up, 1)
            pool.memset(cov_sum[:, :, :], 0.0).then_inc(set_up, 1)
            pool.wait_ge(set_up, 6)

            def pair_rows(b, t):
                i = t % HALF
                pool.wait_ge(x_landed[i], (b * 2 + t // HALF + 1) * 16)
                before = max([p for p in PAIRED if p < t] or [PAIRED[-1] - TILES])
                wait(pool, pooled_s, b * TILES + before + 1)
                rows = slots[:, i, :].rearrange("p (a r w) -> p a r w", r=POOL, w=W)
                pool.tensor_tensor(paired_rows.rearrange("p (a r w) -> p a r w", r=2, w=W),
                                   rows[:, :, 0:2, :], rows[:, :, 2:4, :], ALU.add)\
                    .then_inc(paired, 1)

            def group_norm(b, h):
                n = 2 * b + h
                pool.wait_ge(sums_ready, n + 1)
                pool.tensor_tensor(mean_c, sums[:, h, :], per_pixel, ALU.mult)\
                    .then_inc(mean_ready, 1)
                pool.wait_ge(squared, b * TILES + (h + 1) * HALF)
                pool.tensor_tensor(var_c, sumsq[:, h, :], per_pixel, ALU.mult)
                pool.drain()
                pool.tensor_tensor(sq_c, mean_c, first[:, h, :], ALU.subtract)
                pool.drain()
                pool.tensor_tensor(sq_c, sq_c, sq_c, ALU.mult)
                pool.drain()
                pool.tensor_tensor(var_c, var_c, sq_c, ALU.subtract)
                pool.drain()
                pool.wait_ge(dev_ready, n + 1)
                pool.tensor_tensor(sq_c, dev, dev, ALU.mult)
                pool.tensor_tensor(neg_mean, dev, mean_c, ALU.subtract)
                pool.drain()
                pool.tensor_tensor(sq_c, sq_c, var_c, ALU.add).then_inc(sq_ready, 1)
                pool.wait_ge(var_ready, n + 1)
                pool.tensor_tensor(rstd, v_eps, minus_half, ALU.pow)
                pool.drain()
                pool.tensor_scalar(scale16, rstd, 1.0 / (POOL * POOL), 0.0, ALU.mult, ALU.add)
                pool.tensor_tensor(shift_c, neg_mean, rstd, ALU.mult)
                pool.drain()
                for i in range(HALF):
                    last = pool.tensor_scalar(pooled[:, h, i, :], pooled[:, h, i, :],
                                              scale16[:, i:i + 1], shift_c[:, i:i + 1],
                                              ALU.mult, ALU.add)
                last.then_inc(xn_ready, 1)
                pool.drain()

            def body(b, tiles, at, rest):
                if tiles:
                    pair_rows(b, 0)
                if at:
                    group_norm(b - 1, 1)
                if tiles:
                    for t in PAIRED[1:]:
                        if t > HALF and PAIRED[PAIRED.index(t) - 1] <= HALF:
                            group_norm(b, 0)
                        pair_rows(b, t)

            bodies(pool, body)

            pool.wait_ge(cov_done, B)
            pool.wait_ge(con_landed, 16)
            pool.tensor_tensor(up[:, :, :], rows_f.unsqueeze(2).to_broadcast([P, H, W]),
                               cols_f.unsqueeze(1).to_broadcast([P, H, W]), ALU.mult)\
                .then_inc(up_ready, 1)
            pool.wait_ge(att_copied, B)
            pool.tensor_copy(att_now[:, :, :], att[:, B - 1, :, :]).then_inc(att_now_ready, 1)
            pool.wait_ge(bn_var_ready, 1)
            pool.tensor_tensor(bn_rstd, bn_var, bn_half, ALU.pow).then_inc(bn_rstd_ready, 1)
            with pool.Fori(1, B) as k:
                pool.wait_ge(low_done, k * TILES)
                pool.tensor_copy(att_now[:, :, :], att[:, bass.ds(k - 1, 1), :, :].rearrange(
                    "p o c n -> p (o c) n")).then_inc(att_now_ready, 1)

        @block.scalar
        def _(act):
            act.dma_start(w_stage, w_qkv.rearrange("(o p) n -> p o n", p=P)).then_inc(wq_landed, 16)
            act.dma_start(con[:, :], consts).then_inc(con_landed, 16)
            act.dma_start(wp_n[:, :, :], w_proj.rearrange("(o p) n -> p o n", p=P))\
                .then_inc(wp_landed, 16)
            with nc.allow_non_contiguous_dma(reason="a few KiB once"):
                act.dma_start(temp[:, :], temperature.rearrange("h a b -> (a b) h")
                              .to_broadcast([P, HEADS])).then_inc(wp_landed, 16)
                act.dma_start(gam[:, :], gamma.rearrange("(o p) -> p o", p=P))\
                    .then_inc(wp_landed, 16)
                act.dma_start(bet[:, :], beta.rearrange("(o p) -> p o", p=P))\
                    .then_inc(wp_landed, 16)

            def square(b, t):
                h, i = divmod(t, HALF)
                act.wait_ge(x_landed[i], (b * 2 + h + 1) * 16)
                if i == 0:
                    wait(act, xn_ready, 2 * (b - 1) + h + 1)
                wait(act, squared, b * TILES + t - 1)
                act.activation(junk[:, t % 2, :], slots[:, i, :], ACT.Square, bias=slots[:, i, 0:1],
                               scale=-1.0, accum_out=sumsq[:, h, i:i + 1]).then_inc(squared, 1)

            def exps(a, k):
                n = a * ROUNDS + k
                act.wait_ge(max_ready, n + 1)
                if k > 0:
                    act.wait_ge(e_turned, n)
                for u in range(2):
                    for lc in range(LC):
                        last = act.activation(
                            e_sb[:, u, lc, :], bank(3 + u)[:, lc * POS:(lc + 1) * POS],
                            ACT.Exp, bias=neg_max[:, u * LC + lc:u * LC + lc + 1],
                            accum_out=row_sum[:, lc, 2 * k + u:2 * k + u + 1])
                last.then_inc(exp_done, 1)

            def body(b, tiles, at, rest):
                a, c = b - 1, b - 2
                for t in range(TILES):
                    if rest and t == 4:
                        act.wait_ge(gram_done, c + 1)
                        act.activation(g_sb, bank(4), ACT.Copy).then_inc(gram_copied, 1)
                    if at and t == 4:
                        act.wait_ge(norm_ready, a + 1)
                        act.activation(rnorm, norm2, ACT.Sqrt).then_inc(norm_root, 1)
                    if tiles:
                        square(b, t)
                    if rest and t == ROUND_STEP[3]:
                        exps(c, 3)
                    if at and t in ROUND_STEP[:3]:
                        exps(a, ROUND_STEP.index(t))
                    if rest and t == 3:
                        act.wait_ge(at_turned, c + 1)
                        for cc in range(CC):
                            dst = att[:, bass.ds(c, 1), cc, :].rearrange("p o n -> p (o n)")
                            last = act.activation(dst, bank(6)[:, cc * POS:(cc + 1) * POS],
                                                  ACT.Copy, accum_out=mu[:, bass.ds(c, 1), cc])
                        last.then_inc(att_copied, 1)
                    if at and t == 3:
                        act.wait_ge(qkv_part, TILES * (a + 1))
                        act.activation(qk_sq, bank(0, 2), ACT.Square).then_inc(qk_squared, 1)
                    if at and t == 4:
                        act.wait_ge(qk_turned, a + 1)
                        q_bank = bank(5).rearrange("p (c n) -> p c n", c=CC)
                        for g in range(P // DH):
                            rows = slice(g * DH, (g + 1) * DH)
                            act.activation(q_m[rows, :, g, :], q_bank[rows, :, :], ACT.Copy)
                        act.activation(k_t, bank(6), ACT.Copy).then_inc(qk_copied, 1)

            bodies(act, body)

            def low_copy(n, i, waits=True):
                act.wait_ge(low_done, n + 1)
                wait(act, upsampled, (n - 1) * UNITS)
                act.activation(low_t[:, i, :, :], bank(6)[:, 0:3 * P]
                               .rearrange("p (w n) -> p w n", w=3), ACT.Copy)\
                    .then_inc(low_copied, 1)

            def scale_item(k, last_item):
                for s in range(SLOTS):
                    n = k * SLOTS + s
                    if not (last_item and s == SLOTS - 1):
                        low_copy(n + 1, (s + 1) % 2)
                    o = (s + 4) % TILES
                    for u in range(UNITS):
                        act.wait_ge(upsampled, n * UNITS + u + 1)
                        act.activation(bank(2 * u, 2), bank(2 * u, 2), ACT.Identity,
                                       bias=bn_shift[:, o:o + 1], scale=bn_scale[:, o:o + 1])\
                            .then_inc(scaled, 1)

            low_copy(0, 0)
            act.wait_ge(bn_ready, 1)
            scale_item(0, False)
            with act.Fori(1, B - 1) as k:
                scale_item(k, False)
            scale_item(B - 1, True)

        @block.vector
        def _(dve):
            for n in range(TILES):
                dve.wait_ge(w_turned, n + 1)
                dve.tensor_copy(w_t[:, n, :], bank(2 * (n % 2), 2)[:, 0:768]).then_inc(w_copied, 1)
            for n in range(2 * CC):
                dve.wait_ge(w_turned, TILES + n + 1)
                cc, g = divmod(n, 2)
                dve.tensor_copy(wp_t[:, cc, g * 512:(g + 1) * 512], bank(4 + n % 2))\
                    .then_inc(w_copied, 1)

            def pool_tile(b, t):
                h, i = divmod(t, HALF)
                wait(dve, qkv_part, (b - 1) * TILES + t + 1)
                dst = pooled[:, h, i, :].rearrange("p (a b) -> p a b", a=LOW)
                dve.wait_ge(x_landed[i], (2 * b + h + 1) * 16)
                dve.tensor_copy(first[:, h, i:i + 1], slots[:, i, 0:1])
                if t in PAIRED:
                    dve.wait_ge(paired, b * len(PAIRED) + PAIRED.index(t) + 1)
                    src = paired_rows.rearrange("p (a r b c) -> p a b r c", a=LOW, r=2, b=LOW)
                else:
                    src = slots[:, i, :].rearrange("p (a r b c) -> p a b r c", a=LOW, r=POOL, b=LOW)
                dve.tensor_reduce(dst, src, AX.XY, ALU.add).then_inc(pooled_s, 1)

            def half_sums(b, h):
                dve.wait_ge(pooled_s, b * TILES + (h + 1) * HALF)
                dve.tensor_reduce(sums[:, h, :], pooled[:, h, :, :], AX.X, ALU.add)\
                    .then_inc(sums_ready, 1)

            def half_dev(b, h):
                dve.wait_ge(group_mean, 2 * b + h + 1)
                dve.tensor_tensor(dev, mean_c, bank(7)[:, 256:256 + HALF], ALU.subtract)\
                    .then_inc(dev_ready, 1)

            def half_var(b, h):
                dve.wait_ge(group_var, 2 * b + h + 1)
                dve.tensor_scalar(v_eps, bank(7)[:, 256:256 + HALF], 1.0, EPS_GN, ALU.mult, ALU.add)\
                    .then_inc(var_ready, 1)

            def round_max(a, k):
                n = a * ROUNDS + k
                dve.wait_ge(scored, n + 1)
                if k > 0:
                    dve.wait_ge(exp_done, n)
                dve.tensor_reduce(neg_max[:, :], bank(3, 2).rearrange("p (g m) -> p g m", m=POS),
                                  AX.X, ALU.max, negate=True).then_inc(max_ready, 1)

            def round_copy(a, k):
                n = a * ROUNDS + k
                dve.wait_ge(e_turned, n + 1)
                if k > 0:
                    dve.wait_ge(mixed, n)
                dve.tensor_copy(scratch[:, 1024:2048], bank(5, 2)).then_inc(e_copied, 1)

            def body(b, tiles, at, rest):
                a, c = b - 1, b - 2
                for t in range(TILES):
                    if rest and t == 3:
                        dve.wait_ge(o_turned, c + 1)
                        dve.tensor_tensor(
                            scratch[:, 2048:2560].rearrange("p (g d) -> p g d", d=DH),
                            bank(5).rearrange("p (g d) -> p g d", d=DH),
                            row_inv[:, :, :].rearrange("p l h -> p (l h)").unsqueeze(2)
                            .to_broadcast([P, LC * HEADS, DH]), ALU.mult).then_inc(at_ready, 1)
                    if at and t == 0:
                        half_dev(a, 1)
                    if tiles and t == 4:
                        half_dev(b, 0)
                    if at and t == 4:
                        dve.wait_ge(norm_root, a + 1)
                        dve.reciprocal(rnorm, rnorm)
                        dve.drain()
                        r4 = rnorm.rearrange("p (l s h) -> p l s h", l=LC, s=2)
                        for lc in range(LC):
                            dve.tensor_tensor(r4[:, lc, 1, :], r4[:, lc, 1, :], temp[:, :], ALU.mult)
                        dve.drain()
                        dve.tensor_tensor(
                            scratch[:, 1024:2048].rearrange("p (g d) -> p g d", d=DH),
                            bank(0, 2).rearrange("p (g d) -> p g d", d=DH),
                            rnorm.unsqueeze(2).to_broadcast([P, 2 * LC * HEADS, DH]), ALU.mult)\
                            .then_inc(qk_scaled, 1)
                    if tiles:
                        pool_tile(b, t)
                    if at and t == 0:
                        half_var(a, 1)
                    if tiles and t == 4:
                        half_var(b, 0)
                    if tiles and t == 3:
                        half_sums(b, 0)
                    if tiles and t == 7:
                        half_sums(b, 1)
                    if rest and t == 0:
                        round_max(c, 3)
                        round_copy(c, 2)
                    if rest and t == 1:
                        round_copy(c, 3)
                    if at and t >= 5:
                        round_max(a, t - 5)
                        if t > 5:
                            round_copy(a, t - 6)
                    if rest and t == 2:
                        dve.wait_ge(mixed, (c + 1) * ROUNDS)
                        dve.tensor_copy(o_sb, bank(7).rearrange("p (c n) -> p c n", c=CC))\
                            .then_inc(o_copied, 1)
                        dve.wait_ge(exp_done, (c + 1) * ROUNDS)
                        dve.reciprocal(row_inv[:, :, :], row_sum[:, :, :])
                        dve.drain()
                    if rest and t == 3:
                        dve.wait_ge(at_mean, c + 1)
                        dve.tensor_tensor(a_c, a_t, bank(3)[:, 0:TD].unsqueeze(1)
                                          .to_broadcast([P, LC, TD]), ALU.subtract)\
                            .then_inc(ac_ready, 1)
                    if at and t == 3:
                        dve.wait_ge(qkv_part, TILES * (a + 1))
                        dve.tensor_copy(v_sb, bank(2).rearrange("p (l n) -> p l n", l=LC))
                        dve.wait_ge(qk_squared, a + 1)
                        dve.tensor_reduce(norm2, qk_sq.rearrange("p (g d) -> p g d", d=DH), AX.X,
                                          ALU.add)
                        dve.drain()
                        dve.tensor_scalar(norm2, norm2, EPS_NORM ** 2, None, ALU.max)\
                            .then_inc(norm_ready, 1)
                    if rest and t == 4:
                        dve.wait_ge(cov_done, c + 1)
                        dve.tensor_tensor(cov_sum[:, :, :], cov_sum[:, :, :], bank(3).rearrange(
                            "p (c n) -> p c n", c=CC), ALU.add).then_inc(cov_added, 1)

            dve.wait_ge(set_up, 6)
            dve.wait_ge(wp_landed, 64)
            bodies(dve, body)

            dve.wait_ge(att_copied, B)
            for cc in range(CC):
                dve.tensor_reduce(cov[:, cc, TD:TD + 1], mu[:, :, cc], AX.X, ALU.add)
            dve.drain()
            for cc in range(CC):
                dve.tensor_scalar(cov[:, cc, TD:TD + 1], cov[:, cc, TD:TD + 1], 1.0 / (B * POS),
                                  None, ALU.mult)
                dve.tensor_scalar(mu_d[:, cc, :], mu[:, :, cc], 1.0 / POS, None, ALU.mult)
            dve.drain()
            for cc in range(CC):
                last = dve.tensor_scalar(mu_d[:, cc, :], mu_d[:, cc, :], cov[:, cc, TD:TD + 1],
                                         1.0 / float(np.sqrt(B)), ALU.subtract, ALU.mult)
            last.then_inc(mu_ready, 1)
            dve.wait_ge(mu_turned, 1)
            dve.tensor_copy(mu_dt[:, :], bank(0)[0:B, 0:TD]).then_inc(mu_copied, 1)
            dve.wait_ge(mu_outer, 1)
            dve.wait_ge(cov_added, B)
            dve.tensor_tensor(cov[:, :, 0:TD], cov_sum[:, :, :], bank(1).rearrange(
                "p (c n) -> p c n", c=CC), ALU.add).then_inc(cov_ready, 1)
            for o in range(TILES):
                dve.wait_ge(cov_w, o + 1)
                wait(dve, bn_read, o - 1)
                dve.tensor_copy(bn_mean[:, o:o + 1], bank(2 + o % 4)[:, TD:TD + 1])
                last = dve.tensor_tensor_reduce(
                    out=prod[:, o % 2, :], in0=bank(2 + o % 4)[:, 0:TD], in1=wp_n[:, o, :], scale=1.0,
                    scalar=0.0, op0=ALU.mult, op1=ALU.add, accum_out=bn_var[:, o:o + 1])
                last.then_inc(bn_read, 1)
            dve.wait_ge(bn_read, TILES)
            dve.tensor_scalar(bn_var, bn_var, 0.0, EPS_BN, ALU.max, ALU.add)\
                .then_inc(bn_var_ready, 1)
            dve.wait_ge(bn_rstd_ready, 1)
            dve.tensor_tensor(bn_scale, bn_rstd, gam[:, :], ALU.mult)
            dve.drain()
            dve.tensor_tensor(bn_mean, bn_mean, bn_scale, ALU.mult)
            dve.drain()
            dve.tensor_tensor(bn_shift, bet[:, :], bn_mean, ALU.subtract).then_inc(bn_ready, 1)

            def add_item(k):
                for s in range(SLOTS):
                    if s < HALF:
                        dve.wait_ge(x_landed[s], (k + 2 * B) * 16)
                    else:
                        dve.wait_ge(x_landed[s], (k + 1) * 16)
                    for u in range(UNITS):
                        dve.wait_ge(scaled, (k * SLOTS + s) * UNITS + u + 1)
                        part = slots[:, s, u * UNIT:(u + 1) * UNIT]
                        dve.tensor_tensor(part, part, bank(2 * u, 2), ALU.add).then_inc(added, 1)

            add_item(0)
            with dve.Fori(1, B) as k:
                add_item(k)

        @block.tensor
        def _(pe):
            pe.wait_ge(con_landed, 16)
            pe.wait_ge(wq_landed, 16)
            for j in range(TILES):
                if j >= 2:
                    pe.wait_ge(w_copied, j - 1)
                for o in range(6):
                    last = pe.transpose(bank(2 * (j % 2), 2)[:, o * P:(o + 1) * P],
                                        w_stage[:, o, j * P:(j + 1) * P], ident)
                last.then_inc(w_turned, 1)
            pe.wait_ge(wp_landed, 64)
            for n in range(2 * CC):
                if n >= 2:
                    pe.wait_ge(w_copied, TILES + n - 1)
                cc, g = divmod(n, 2)
                for o in range(4):
                    last = pe.transpose(bank(4 + n % 2)[:, o * P:(o + 1) * P],
                                        wp_n[:, 4 * g + o, cc * P:(cc + 1) * P], ident)
                last.then_inc(w_turned, 1)
            pe.wait_ge(set_up, 6)
            pe.wait_ge(w_copied, TILES + 2 * CC)

            def group_means(b, h):
                pe.wait_ge(mean_ready, 2 * b + h + 1)
                pe.matmul(bank(7)[:, 256:256 + HALF], lhsT=group, rhs=mean_c, start=True,
                          stop=True, skip_group_check=True).then_inc(group_mean, 1)

            def group_vars(b, h):
                pe.wait_ge(sq_ready, 2 * b + h + 1)
                pe.matmul(bank(7)[:, 256:256 + HALF], lhsT=group, rhs=sq_c, start=True,
                          stop=True, skip_group_check=True).then_inc(group_var, 1)

            def qkv(b, j):
                h, i = divmod(j, HALF)
                if i == 0:
                    pe.wait_ge(xn_ready, 2 * b + h + 1)
                if j == 0:
                    wait(pe, qk_scaled, b)
                for lc in range(LC):
                    lhs = pooled[:, h, i, lc * P:(lc + 1) * P]
                    pe.matmul(bank(lc), lhsT=lhs, rhs=w_t[:, j, 0:2 * TD], start=(j == 0),
                              stop=(j == TILES - 1), skip_group_check=True)
                    last = pe.matmul(bank(2)[:, lc * TD:(lc + 1) * TD], lhsT=lhs,
                                     rhs=w_t[:, j, 2 * TD:3 * TD], start=(j == 0 and lc == 0),
                                     stop=(j == TILES - 1), skip_group_check=True)
                last.then_inc(qkv_part, 1)

            def scores(a, k, before):
                n = a * ROUNDS + k
                if k == 0:
                    pe.wait_ge(qk_copied, a + 1)
                    if before:
                        pe.wait_ge(cov_added, a)
                else:
                    pe.wait_ge(exp_done, n)
                for u in range(2):
                    cc, g = divmod(2 * k + u, P // DH)
                    for lc in range(LC):
                        last = pe.matmul(bank(3 + u)[:, lc * POS:(lc + 1) * POS],
                                         lhsT=q_m[:, cc, g, lc * P:(lc + 1) * P],
                                         rhs=k_t[:, cc, :], start=True, stop=True,
                                         skip_group_check=True)
                last.then_inc(scored, 1)

            def turn_e(a, k):
                n = a * ROUNDS + k
                pe.wait_ge(exp_done, n + 1)
                if k > 0:
                    pe.wait_ge(e_copied, n)
                for u in range(2):
                    for lc in range(LC):
                        for mc in range(LC):
                            last = pe.transpose(
                                bank(5 + u)[:, mc * POS + lc * P:mc * POS + (lc + 1) * P],
                                e_sb[:, u, lc, mc * P:(mc + 1) * P], ident)
                last.then_inc(e_turned, 1)

            def mix(a, k):
                pe.wait_ge(e_copied, a * ROUNDS + k + 1)
                for u in range(2):
                    hd = 2 * k + u
                    cc, r = divmod(hd * DH, P)
                    for mc in range(LC):
                        last = pe.matmul(bank(7)[r:r + DH, cc * POS:(cc + 1) * POS],
                                         lhsT=v_sb[:, mc, hd * DH:(hd + 1) * DH],
                                         rhs=e_t[:, u, mc, :], start=(mc == 0),
                                         stop=(mc == LC - 1), skip_group_check=True)
                last.then_inc(mixed, 1)

            def body(b, tiles, at, rest):
                a, c = b - 1, b - 2
                for t in range(TILES):
                    if t == 0:
                        if at:
                            group_means(a, 1)
                        if rest:
                            turn_e(c, 2)
                        if at:
                            group_vars(a, 1)
                        if rest:
                            scores(c, 3, True)
                        if at:
                            qkv(a, 3)
                        if rest:
                            if at:
                                pe.wait_ge(var_ready, 2 * a + 2)
                            mix(c, 1)
                    if t == 1:
                        if rest:
                            turn_e(c, 3)
                            mix(c, 2)
                        if at:
                            qkv(a, 4)
                            qkv(a, 5)
                    if t == 2:
                        if rest:
                            mix(c, 3)
                        if at:
                            qkv(a, 6)
                            qkv(a, 7)
                        if rest:
                            pe.wait_ge(o_copied, c + 1)
                            for lc in range(LC):
                                for cc in range(CC):
                                    last = pe.transpose(
                                        bank(5)[:, lc * TD + cc * P:lc * TD + (cc + 1) * P],
                                        o_sb[:, cc, lc * P:(lc + 1) * P], ident)
                            last.then_inc(o_turned, 1)
                    if t == 3 and rest:
                        pe.wait_ge(at_ready, c + 1)
                        for lc in range(LC):
                            last = pe.matmul(bank(3)[:, 0:TD], lhsT=ones[:, :], rhs=a_t[:, lc, :],
                                             start=(lc == 0), stop=(lc == LC - 1))
                        last.then_inc(at_mean, 1)
                        for cc in range(CC):
                            for lc in range(LC):
                                last = pe.transpose(
                                    bank(6)[:, cc * POS + lc * P:cc * POS + (lc + 1) * P],
                                    a_t[:, lc, cc * P:(cc + 1) * P], ident)
                        last.then_inc(at_turned, 1)
                    if t == 3 and tiles:
                        group_means(b, 0)
                    if t == 3 and rest:
                        pe.wait_ge(ac_ready, c + 1)
                        for lo in range(LC):
                            for lc in range(LC):
                                last = pe.matmul(bank(4)[:, lo * TD:(lo + 1) * TD],
                                                 lhsT=gram[:, lc, lo * P:(lo + 1) * P],
                                                 rhs=a_c[:, lc, :], start=(lc == 0),
                                                 stop=(lc == LC - 1), skip_group_check=True)
                        last.then_inc(gram_done, 1)
                    if t == 4:
                        if tiles:
                            group_vars(b, 0)
                        if rest:
                            pe.wait_ge(gram_copied, c + 1)
                            for cc in range(CC):
                                for lc in range(LC):
                                    last = pe.matmul(bank(3)[:, cc * TD:(cc + 1) * TD],
                                                     lhsT=a_c[:, lc, cc * P:(cc + 1) * P],
                                                     rhs=g_sb[:, lc, :], start=(lc == 0),
                                                     stop=(lc == LC - 1), skip_group_check=True)
                            last.then_inc(cov_done, 1)
                        if at:
                            pe.wait_ge(qk_scaled, a + 1)
                            if rest:
                                pe.wait_ge(att_copied, c + 1)
                            for s in range(2):
                                for cc in range(CC):
                                    for lc in range(LC):
                                        last = pe.transpose(
                                            bank(5 + s)[:, cc * POS + lc * P:cc * POS + (lc + 1) * P],
                                            qk_n[:, lc, s * TD + cc * P:s * TD + (cc + 1) * P], ident)
                            last.then_inc(qk_turned, 1)
                    if t >= 5:
                        k = t - 5
                        if at and k > 0:
                            turn_e(a, k - 1)
                        if at:
                            scores(a, k, rest)
                        if at and k == 2:
                            mix(a, 0)
                        if tiles:
                            qkv(b, k)

            bodies(pe, body)

            pe.wait_ge(mu_ready, 1)
            for cc in range(CC):
                last = pe.transpose(bank(0)[0:B, cc * P:(cc + 1) * P], mu_d[:, cc, :], ident)
            last.then_inc(mu_turned, 1)
            pe.wait_ge(mu_copied, 1)
            for cc in range(CC):
                last = pe.matmul(bank(1)[:, cc * TD:(cc + 1) * TD],
                                 lhsT=mu_dt[:, cc * P:(cc + 1) * P], rhs=mu_dt[:, :], start=True,
                                 stop=True, skip_group_check=True)
            last.then_inc(mu_outer, 1)
            pe.wait_ge(cov_ready, 1)
            for o in range(TILES):
                if o >= 4:
                    pe.wait_ge(bn_read, o - 3)
                for cc in range(CC):
                    last = pe.matmul(bank(2 + o % 4)[:, 0:TD + 1],
                                     lhsT=wp_t[:, cc, o * P:(o + 1) * P], rhs=cov[:, cc, :],
                                     start=(cc == 0), stop=(cc == CC - 1))
                last.then_inc(cov_w, 1)

            def project(n, s, fresh):
                o = (s + 4) % TILES
                if fresh is not None:
                    pe.wait_ge(att_now_ready, fresh)
                wait(pe, added, (n - 1) * UNITS)
                wait(pe, low_copied, n)
                for w, row in enumerate(WINDOWS):
                    for cc in range(CC):
                        last = pe.matmul(bank(6)[:, w * P:(w + 1) * P],
                                         lhsT=att_now[:, cc, row * LOW:row * LOW + P],
                                         rhs=wp_t[:, cc, o * P:(o + 1) * P], start=(cc == 0),
                                         stop=(cc == CC - 1), skip_group_check=True)
                last.then_inc(low_done, 1)

            def upsample_item(k, last_item):
                for s in range(SLOTS):
                    n = k * SLOTS + s
                    if s < SLOTS - 1:
                        project(n + 1, s + 1, None)
                    elif not last_item:
                        project(n + 1, 0, k + 2)
                    pe.wait_ge(low_copied, n + 1)
                    for u in range(UNITS):
                        wait(pe, added, (n - 1) * UNITS + u + 1)
                        if u == 3 and not (last_item and s == SLOTS - 1):
                            pe.wait_ge(low_copied, n + 2)
                        for v in range(2):
                            blk = 2 * u + v
                            last = pe.matmul(bank(blk), lhsT=low_t[:, s % 2, WINDOW_OF[blk], :],
                                             rhs=up[:, blk * 8:(blk + 1) * 8, :], start=True,
                                             stop=True)
                        last.then_inc(upsampled, 1)

            pe.wait_ge(bn_read, TILES)
            project(0, 0, 1)
            pe.wait_ge(up_ready, 1)
            upsample_item(0, False)
            with pe.Fori(1, B - 1) as k:
                upsample_item(k, False)
            upsample_item(B - 1, True)


_INS = ["x", "L0_conv_w_qkv", "L0_conv_temperature", "L0_conv_w_proj", "L0_conv_bn_gamma",
        "L0_conv_bn_beta"]


def kernel(**inputs):
    import concourse.bacc as bacc
    from concourse.bass_utils import run_bass_kernel_spmd

    nc = bacc.Bacc("TRN2", target_bir_lowering=False, num_devices=1)
    arrays, args = {}, []
    for name in _INS:
        a = np.ascontiguousarray(inputs[name])
        arrays[f"in_{name}"] = a
        args.append(nc.dram_tensor(f"in_{name}", a.shape, mybir.dt.from_np(a.dtype),
                                   kind="ExternalInput").ap())
    table = constants()
    arrays["tables"] = table
    tab = nc.dram_tensor("tables", table.shape, F32, kind="ExternalInput").ap()
    out = nc.dram_tensor("out", (B, CH, H, W), F32, kind="ExternalOutput").ap()
    program(nc, *args, tab, out)
    r = run_bass_kernel_spmd(nc, [arrays], core_ids=[0])
    return r.results[0]["out"]
```

```python
from contextlib import ExitStack

import numpy as np

import concourse.bass as bass
from concourse import mybir

F32 = mybir.dt.float32
U8 = mybir.dt.uint8
ALU = mybir.AluOpType
ACT = mybir.ActivationFunctionType
AX = mybir.AxisListType

P = 128
B, CH, H, W = 16, 1024, 64, 64
LOW = 16
POOL = H // LOW
PIX = H * W
POS = LOW * LOW
TILES = CH // P
HALF = TILES // 2
GROUP = CH // 32
HEADS, DH = 8, 32
TD = HEADS * DH
CC = TD // P
LC = POS // P
EPS_GN, EPS_BN, EPS_NORM = 1e-5, 1e-5, 1e-12
PAIRED = (0, 2, 3, 4, 6, 7)
PAIR_HEADS = 2
ROUNDS = HEADS // PAIR_HEADS
WINDOWS = (0, 5, 8)
WINDOW_OF = (0, 0, 0, 1, 1, 1, 2, 2)
SLOTS = 8
UNIT = 1024
UNITS = PIX // UNIT
BN_FIRST = (HALF, 0)


def bilinear():
    src = (np.arange(H) + 0.5) / POOL - 0.5
    m = np.maximum(0.0, 1.0 - np.abs(src[:, None] - np.arange(LOW)[None, :]))
    return m / m.sum(1, keepdims=True)


def constants():
    u = bilinear()
    p = np.arange(P)
    ident = np.eye(P)
    group = (p[:, None] // GROUP == p[None, :] // GROUP) / GROUP
    gram = np.kron(u.T @ u, u.T @ u) / (B * PIX)
    gram = gram.reshape(LC, P, POS).transpose(1, 0, 2).reshape(P, LC * POS)
    rows = np.zeros((P, H))
    for r in range(H):
        rows[:, r] = u[r, WINDOWS[WINDOW_OF[r // 8]] + p // LOW]
    cols = u[:, p % LOW].T
    return np.concatenate([ident, group, gram, rows, cols], axis=1).astype(np.float32)


C_IDENT, C_GROUP, C_GRAM, C_ROWS, C_COLS, C_END = 0, 128, 256, 768, 832, 896


def program(nc, x, w_qkv, temperature, w_proj, gamma, beta, consts, out):
    x_rows = x.rearrange("b c h w -> (b c) (h w)")
    out_rows = out.rearrange("b c h w -> (b c) (h w)")

    def tile_rows(rows, b, j):
        return rows[bass.ds(b * CH + j * P, P), :]

    with ExitStack() as ctx:
        def sb(name, shape, dt=F32):
            return ctx.enter_context(nc.sbuf_tensor(name, shape, dt))

        def sem(name):
            return ctx.enter_context(nc.semaphore(name))

        slots = sb("slots", [P, SLOTS, PIX])
        late = slots[:, 4:8, :].rearrange("p s n -> p (s n)")
        w_t = late[:, 0:6144].rearrange("p (j n) -> p j n", j=TILES)
        pooled = late[:, 6144:8192].rearrange("p (h i n) -> p h i n", h=2, i=HALF)
        junk = late[:, 8192:10240].bitcast(U8).rearrange("p (k n) -> p k n", k=2)
        q_m = late[:, 12288:14336].rearrange("p (c g n) -> p c g n", c=CC, g=P // DH)
        k_t = late[:, 14336:14848].rearrange("p (c n) -> p c n", c=CC)
        v_sb = late[:, 14848:15360].rearrange("p (l n) -> p l n", l=LC)
        o_sb = late[:, 15360:15872].rearrange("p (c n) -> p c n", c=CC)
        up = sb("up", [P, H, W])
        scratch = up[:, :, :].rearrange("p a b -> p (a b)")
        e_sb = scratch[:, 0:1024].rearrange("p (h l m) -> p h l m", h=2, l=LC)
        e_t = scratch[:, 1024:2048].rearrange("p (h m l) -> p h m l", h=2, m=LC)
        qk_sq = scratch[:, 0:1024]
        qk_n = scratch[:, 1024:2048].rearrange("p (l n) -> p l n", l=LC)
        a_t = scratch[:, 2048:2560].rearrange("p (l n) -> p l n", l=LC)
        a_c = scratch[:, 2560:3072].rearrange("p (l n) -> p l n", l=LC)
        g_sb = scratch[:, 3072:3584].rearrange("p (l n) -> p l n", l=LC)
        att = sb("att", [P, B, CC, POS])
        w_stage = att[:, :, :, :].rearrange("p b c n -> p (b c n)")[:, 0:6144]\
            .rearrange("p (o n) -> p o n", o=6)
        wp_t = sb("wp_t", [P, CC, CH])
        wp_n = sb("wp_n", [P, TILES, TD])
        shared = sb("shared", [P, 2050])
        paired_rows = (late[:, 10240:12288], shared[:, 0:2048])
        low_t = shared[:, 0:768].rearrange("p (i w n) -> p i w n", i=2, w=3)
        att_now = shared[:, 768:1280].rearrange("p (c n) -> p c n", c=CC)
        cov = shared[:, 1280:1794].rearrange("p (c n) -> p c n", c=CC)
        mu_dt = shared[0:B, 1794:2050]
        con = sb("con", [P, C_END])
        ident, group = con[:, C_IDENT:C_GROUP], con[:, C_GROUP:C_GRAM]
        gram = con[:, C_GRAM:C_ROWS].rearrange("p (l n) -> p l n", l=LC)
        rows_f, cols_f = con[:, C_ROWS:C_COLS], con[:, C_COLS:C_END]
        ones = sb("ones", [P, P])
        cov_sum = sb("cov_sum", [P, CC, TD])
        temp = sb("temp", [P, HEADS])
        gam, bet = sb("gam", [P, TILES]), sb("bet", [P, TILES])
        first = sb("first", [P, 2, HALF])
        sumsq = sb("sumsq", [P, 2, HALF])
        sums = sb("sums", [P, 2, HALF])
        gs = sb("gs", [P, 11, HALF])
        mean_c, dev, var_c, sq_c, v_eps, rstd, scale16, shift_c, neg_mean, minus_half, \
            per_pixel = (gs[:, i, :] for i in range(11))
        nrm = sb("nrm", [P, 2, 2 * LC * HEADS])
        norm2, rnorm = nrm[:, 0, :], nrm[:, 1, :]
        neg_max = sb("neg_max", [P, 2, 2 * LC])
        row_sum = sb("row_sum", [P, LC, HEADS])
        row_inv = sb("row_inv", [P, LC, HEADS])
        mu = sb("mu", [P, B, CC])
        mu_d = sb("mu_d", [P, CC, B])
        bn = sb("bn", [P, 6, TILES])
        bn_var, bn_mean, bn_rstd, bn_scale, bn_shift, bn_half = (bn[:, i, :] for i in range(6))
        prod = cov_sum
        ps = ctx.enter_context(nc.psum_tensor("ps", [P, 8, 512], F32))

        def bank(n, k=1):
            return ps[:, n:n + k, :].rearrange("p a b -> p (a b)")

        x_landed = [sem(f"x_landed{s}") for s in range(SLOTS)]
        stored = [sem(f"stored{s}") for s in range(SLOTS)]
        wq_landed, wp_landed, con_landed = sem("wq_landed"), sem("wp_landed"), sem("con_landed")
        small_landed = sem("small_landed")
        set_up = sem("set_up")
        w_turned, w_copied = sem("w_turned"), sem("w_copied")
        wp_turned, wp_copied = sem("wp_turned"), sem("wp_copied")
        squared, pooled_s, paired = sem("squared"), sem("pooled"), sem("paired")
        sums_ready, mean_ready, group_mean = sem("sums_ready"), sem("mean_ready"), sem("group_mean")
        dev_ready, sq_ready, group_var = sem("dev_ready"), sem("sq_ready"), sem("group_var")
        var_ready, xn_ready, qkv_part = sem("var_ready"), sem("xn_ready"), sem("qkv_part")
        qk_part = sem("qk_part")
        qk_squared, norm_ready, norm_root = sem("qk_squared"), sem("norm_ready"), sem("norm_root")
        qk_scaled, qk_turned = sem("qk_scaled"), sem("qk_turned")
        qk_copied, scored, max_ready = sem("qk_copied"), sem("scored"), sem("max_ready")
        exp_done, e_turned, e_copied = sem("exp_done"), sem("e_turned"), sem("e_copied")
        mixed, o_copied, o_turned = sem("mixed"), sem("o_copied"), sem("o_turned")
        at_ready, at_mean, at_turned = sem("at_ready"), sem("at_mean"), sem("at_turned")
        att_copied, ac_ready, gram_done = sem("att_copied"), sem("ac_ready"), sem("gram_done")
        gram_copied, cov_done, cov_added = sem("gram_copied"), sem("cov_done"), sem("cov_added")
        mu_ready, mu_turned, mu_copied = sem("mu_ready"), sem("mu_turned"), sem("mu_copied")
        mu_outer, cov_ready, cov_w = sem("mu_outer"), sem("cov_ready"), sem("cov_w")
        bn_read = sem("bn_read")
        bn_var_ready, bn_rstd_ready, bn_ready = sem("bn_var_ready"), sem("bn_rstd"), sem("bn_ready")
        up_ready, att_now_ready = sem("up_ready"), sem("att_now_ready")
        low_done, low_copied = sem("low_done"), sem("low_copied")
        upsampled, scaled, added = sem("upsampled"), sem("scaled"), sem("added")

        def wait(eng, s, value):
            if not (isinstance(value, int) and value <= 0):
                eng.wait_ge(s, value)

        LAST_BANK = (3, 0, 3, 0)

        def bodies(eng, body, heads):
            body(0, True, False, False)
            body(1, True, True, False)
            with eng.Fori(2, B) as b:
                body(b, True, True, True)
            body(B, False, True, True)
            heads()
            body(B + 1, False, False, True)

        block = ctx.enter_context(nc.Block())

        @block.sync
        def _(sp):
            sp.dma_start(w_stage, w_qkv.rearrange("(o p) n -> p o n", p=P)).then_inc(wq_landed, 16)
            sp.dma_start(con[:, :], consts).then_inc(con_landed, 16)

            def load_item(b):
                for t in range(TILES):
                    if isinstance(b, int) and t == 1:
                        sp.dma_start(wp_n[:, :, :], w_proj.rearrange("(o p) n -> p o n", p=P))\
                          .then_inc(wp_landed, 16)
                    wait(sp, pooled_s, b * TILES + t - 3)
                    wait(sp, squared, b * TILES + t - 3)
                    sp.dma_start(slots[:, t % HALF, :], tile_rows(x_rows, b, t)).then_inc(x_landed[t % HALF], 16)

            load_item(0)
            with sp.Fori(1, B) as b:
                load_item(b)
            sp.wait_ge(qkv_part, TILES * B)
            sp.dma_start(slots[:, 4, :], tile_rows(x_rows, B - 1, 0)).then_inc(x_landed[4], 16)
            sp.dma_start(slots[:, 5, :], tile_rows(x_rows, B - 1, 1)).then_inc(x_landed[5], 16)
            sp.wait_ge(pooled_s, TILES * B)
            sp.wait_ge(squared, TILES * B)
            sp.dma_start(slots[:, 6, :], tile_rows(x_rows, B - 1, 2)).then_inc(x_landed[6], 16)
            sp.wait_ge(o_turned, B)
            sp.dma_start(slots[:, 7, :], tile_rows(x_rows, B - 1, 3)).then_inc(x_landed[7], 16)

            def stores(s, n):
                return (n + (UNITS - 1 if s == 0 else 0)) * 16

            def store(s, b):
                sp.dma_start(tile_rows(out_rows, b, (s + 4) % TILES), slots[:, s, :]).then_inc(stored[s], 16)

            def refill(s, b, n):
                sp.wait_ge(stored[s], stores(s, n))
                sp.dma_start(slots[:, s, :], tile_rows(x_rows, b, (s + 4) % TILES)).then_inc(x_landed[s], 16)

            def store_item(k, b, more):
                for s in range(SLOTS if more else SLOTS - 1):
                    sp.wait_ge(added, (k * SLOTS + s + 1) * UNITS)
                    store(s, b)
                    if s < 2:
                        refill(s + 6, b, k)
                    elif more:
                        refill(s - 2, b + 1, k + 1)

            for u in range(UNITS):
                px = slice(u * UNIT, (u + 1) * UNIT)
                sp.wait_ge(added, u + 1)
                sp.dma_start(tile_rows(out_rows, B - 1, HALF)[:, px], slots[:, 0, px]).then_inc(stored[0], 16)
            refill(0, 0, 1)
            for s in range(1, SLOTS):
                sp.wait_ge(added, (s + 1) * UNITS)
                store(s, B - 1)
                if s == 1:
                    refill(1, 0, 1)
                elif 3 <= s < 6:
                    refill(s - 1, 0, 1)
                elif s == 7:
                    refill(s - 2, 0, 1)
            with sp.Fori(1, B - 1) as k:
                store_item(k, k - 1, True)
            store_item(B - 1, B - 2, False)
            for u in range(UNITS):
                px = slice(u * UNIT, (u + 1) * UNIT)
                sp.wait_ge(added, (B * SLOTS - 1) * UNITS + u + 1)
                sp.dma_start(tile_rows(out_rows, B - 2, 3)[:, px], slots[:, SLOTS - 1, px])\
                  .then_inc(stored[SLOTS - 1], 16)
            for s in range(SLOTS - 1):
                sp.wait_ge(stored[s], stores(s, B))
            sp.wait_ge(stored[SLOTS - 1], 16 * (B - 1 + UNITS))

        @block.gpsimd
        def _(pool):
            pool.memset(q_m, 0.0).then_inc(set_up, 1)
            pool.memset(ones[:, :], 1.0 / POS).then_inc(set_up, 1)
            pool.memset(minus_half, -0.5).then_inc(set_up, 1)
            pool.memset(bn_half, -0.5).then_inc(set_up, 1)
            pool.memset(per_pixel, 1.0 / PIX).then_inc(set_up, 1)
            pool.memset(cov_sum[:, :, :], 0.0).then_inc(set_up, 1)
            pool.wait_ge(set_up, 6)

            def pair_rows(b, t):
                i = t % HALF
                pool.wait_ge(x_landed[i], (b * 2 + t // HALF + 1) * 16)
                n = PAIRED.index(t)
                before = PAIRED[n - 2] - (TILES if n < 2 else 0)
                wait(pool, pooled_s, b * TILES + before + 1)
                rows = slots[:, i, :].rearrange("p (a r w) -> p a r w", r=POOL, w=W)
                pool.tensor_tensor(paired_rows[n % 2].rearrange("p (a r w) -> p a r w", r=2, w=W),
                                   rows[:, :, 0:2, :], rows[:, :, 2:4, :], ALU.add)\
                    .then_inc(paired, 1)

            def group_norm(b, h):
                n = 2 * b + h
                pool.wait_ge(sums_ready, n + 1)
                pool.tensor_tensor(mean_c, sums[:, h, :], per_pixel, ALU.mult)\
                    .then_inc(mean_ready, 1)
                pool.wait_ge(squared, b * TILES + (h + 1) * HALF)
                pool.tensor_tensor(var_c, sumsq[:, h, :], per_pixel, ALU.mult)
                pool.drain()
                pool.tensor_tensor(sq_c, mean_c, first[:, h, :], ALU.subtract)
                pool.drain()
                pool.tensor_tensor(sq_c, sq_c, sq_c, ALU.mult)
                pool.drain()
                pool.tensor_tensor(var_c, var_c, sq_c, ALU.subtract)
                pool.drain()
                pool.wait_ge(dev_ready, n + 1)
                pool.tensor_tensor(sq_c, dev, dev, ALU.mult)
                pool.tensor_tensor(neg_mean, dev, mean_c, ALU.subtract)
                pool.drain()
                pool.tensor_tensor(sq_c, sq_c, var_c, ALU.add).then_inc(sq_ready, 1)
                pool.wait_ge(var_ready, n + 1)
                pool.tensor_tensor(rstd, v_eps, minus_half, ALU.pow)
                pool.drain()
                pool.tensor_scalar(scale16, rstd, 1.0 / (POOL * POOL), 0.0, ALU.mult, ALU.add)
                pool.tensor_tensor(shift_c, neg_mean, rstd, ALU.mult)
                pool.drain()
                for i in range(HALF):
                    last = pool.tensor_scalar(pooled[:, h, i, :], pooled[:, h, i, :],
                                              scale16[:, i:i + 1], shift_c[:, i:i + 1],
                                              ALU.mult, ALU.add)
                last.then_inc(xn_ready, 1)
                pool.drain()

            def body(b, tiles, at, rest):
                if tiles:
                    pair_rows(b, 0)
                if at:
                    group_norm(b - 1, 1)
                if tiles:
                    for t in PAIRED[1:]:
                        if t > HALF and PAIRED[PAIRED.index(t) - 1] <= HALF:
                            group_norm(b, 0)
                        pair_rows(b, t)

            bodies(pool, body, lambda: None)

            def build_up(half):
                rows = slice(half * H // 2, (half + 1) * H // 2)
                pool.tensor_tensor(up[:, rows, :],
                                   rows_f[:, rows].unsqueeze(2).to_broadcast([P, H // 2, W]),
                                   cols_f.unsqueeze(1).to_broadcast([P, H // 2, W]), ALU.mult)\
                    .then_inc(up_ready, 1)

            pool.wait_ge(con_landed, 16)
            pool.wait_ge(mixed, ROUNDS * B)
            build_up(0)
            pool.wait_ge(att_copied, B)
            pool.tensor_copy(att_now, att[:, B - 1, :, :]).then_inc(att_now_ready, 1)
            pool.wait_ge(cov_done, B)
            build_up(1)
            for h in range(2):
                cols = slice(BN_FIRST[h], BN_FIRST[h] + HALF)
                pool.wait_ge(bn_var_ready, h + 1)
                pool.tensor_tensor(bn_rstd[:, cols], bn_var[:, cols], bn_half[:, cols], ALU.pow)\
                    .then_inc(bn_rstd_ready, 1)
            with pool.Fori(1, B) as k:
                pool.wait_ge(low_done, k * TILES)
                pool.tensor_copy(att_now, att[:, bass.ds(k - 1, 1), :, :].rearrange(
                    "p o c n -> p (o c) n")).then_inc(att_now_ready, 1)

        @block.scalar
        def _(act):
            with nc.allow_non_contiguous_dma(reason="a few KiB once"):
                act.dma_start(temp[:, :], temperature.rearrange("h a b -> (a b) h")
                              .to_broadcast([P, HEADS])).then_inc(small_landed, 16)
                act.dma_start(gam[:, :], gamma.rearrange("(o p) -> p o", p=P))\
                    .then_inc(small_landed, 16)
                act.dma_start(bet[:, :], beta.rearrange("(o p) -> p o", p=P))\
                    .then_inc(small_landed, 16)
            for n in range(TILES):
                act.wait_ge(w_turned, n + 1)
                act.activation(w_t[:, n, :], bank(2 * (n % 2), 2)[:, 0:768], ACT.Copy)\
                    .then_inc(w_copied, 1)

            def square(b, t):
                h, i = divmod(t, HALF)
                act.wait_ge(x_landed[i], (b * 2 + h + 1) * 16)
                if i == 0:
                    wait(act, xn_ready, 2 * (b - 1) + h + 1)
                wait(act, squared, b * TILES + t - 1)
                act.activation(junk[:, t % 2, :], slots[:, i, :], ACT.Square, bias=slots[:, i, 0:1],
                               scale=-1.0, accum_out=sumsq[:, h, i:i + 1]).then_inc(squared, 1)

            def exps(a, k, first_bank=3):
                n = a * ROUNDS + k
                act.wait_ge(max_ready, n + 1)
                if k > 0:
                    act.wait_ge(e_turned, n)
                for u in range(2):
                    for lc in range(LC):
                        last = act.activation(
                            e_sb[:, u, lc, :], bank(first_bank + u)[:, lc * POS:(lc + 1) * POS],
                            ACT.Exp, bias=neg_max[:, k % 2, u * LC + lc:u * LC + lc + 1],
                            accum_out=row_sum[:, lc, 2 * k + u:2 * k + u + 1])
                last.then_inc(exp_done, 1)

            def last_heads():
                for k in range(ROUNDS):
                    exps(B - 1, k, LAST_BANK[k])

            def copy_attention(c):
                act.wait_ge(at_turned, c + 1)
                for cc in range(CC):
                    dst = att[:, bass.ds(c, 1), cc, :].rearrange("p o n -> p (o n)")
                    last = act.activation(dst, bank(6)[:, cc * POS:(cc + 1) * POS],
                                          ACT.Copy, accum_out=mu[:, bass.ds(c, 1), cc])
                last.then_inc(att_copied, 1)

            def copy_gram(c):
                act.wait_ge(gram_done, c + 1)
                act.activation(g_sb, bank(4), ACT.Copy).then_inc(gram_copied, 1)

            def copy_qk(a):
                act.wait_ge(qk_turned, a + 1)
                q_bank = bank(5).rearrange("p (c n) -> p c n", c=CC)
                for g in range(P // DH):
                    rows = slice(g * DH, (g + 1) * DH)
                    act.activation(q_m[rows, :, g, :], q_bank[rows, :, :], ACT.Copy)
                act.activation(k_t, bank(6), ACT.Copy).then_inc(qk_copied, 1)

            def body(b, tiles, at, rest):
                a, c = b - 1, b - 2
                if tiles:
                    square(b, 0)
                if rest and at:
                    exps(c, 3)
                if tiles:
                    square(b, 1)
                    square(b, 2)
                    square(b, 3)
                if at:
                    act.wait_ge(qk_part, a + 1)
                    act.activation(qk_sq, bank(0, 2), ACT.Square).then_inc(qk_squared, 1)
                if tiles:
                    square(b, 4)
                if at:
                    act.wait_ge(norm_ready, a + 1)
                    act.activation(rnorm, norm2, ACT.Sqrt).then_inc(norm_root, 1)
                if rest and tiles:
                    copy_gram(c)
                if rest:
                    copy_attention(c)
                if rest and not tiles:
                    copy_gram(c)
                if at:
                    copy_qk(a)
                for k in range(3):
                    if tiles:
                        square(b, 5 + k)
                    if at and tiles:
                        exps(a, k)

            bodies(act, body, last_heads)

            def low_copy(n, i, waits=True):
                act.wait_ge(low_done, n + 1)
                wait(act, upsampled, (n - 1) * UNITS)
                act.activation(low_t[:, i, :, :], bank(6)[:, 0:3 * P]
                               .rearrange("p (w n) -> p w n", w=3), ACT.Copy)\
                    .then_inc(low_copied, 1)

            def scale_item(k, last_item):
                for s in range(SLOTS):
                    n = k * SLOTS + s
                    o = (s + 4) % TILES
                    if isinstance(k, int) and s == HALF:
                        act.wait_ge(bn_ready, 2)
                    for u in range(UNITS):
                        if u == 2 and not (last_item and s == SLOTS - 1):
                            low_copy(n + 1, (s + 1) % 2)
                        act.wait_ge(upsampled, n * UNITS + u + 1)
                        act.activation(bank(2 * u, 2), bank(2 * u, 2), ACT.Identity,
                                       bias=bn_shift[:, o:o + 1], scale=bn_scale[:, o:o + 1])\
                            .then_inc(scaled, 1)

            low_copy(0, 0)
            act.wait_ge(bn_ready, 1)
            scale_item(0, False)
            with act.Fori(1, B - 1) as k:
                scale_item(k, False)
            scale_item(B - 1, True)

        @block.vector
        def _(dve):
            def wp_copy(n):
                dve.wait_ge(wp_turned, n + 1)
                cc, g = divmod(n, 2)
                dve.tensor_copy(wp_t[:, cc, g * 512:(g + 1) * 512], bank(4 + n % 2))\
                    .then_inc(wp_copied, 1)

            def pool_tile(b, t):
                h, i = divmod(t, HALF)
                wait(dve, qkv_part, (b - 1) * TILES + t + 1)
                dst = pooled[:, h, i, :].rearrange("p (a b) -> p a b", a=LOW)
                dve.wait_ge(x_landed[i], (2 * b + h + 1) * 16)
                dve.tensor_copy(first[:, h, i:i + 1], slots[:, i, 0:1])
                if t in PAIRED:
                    dve.wait_ge(paired, b * len(PAIRED) + PAIRED.index(t) + 1)
                    src = paired_rows[PAIRED.index(t) % 2].rearrange("p (a r b c) -> p a b r c", a=LOW, r=2, b=LOW)
                else:
                    src = slots[:, i, :].rearrange("p (a r b c) -> p a b r c", a=LOW, r=POOL, b=LOW)
                dve.tensor_reduce(dst, src, AX.XY, ALU.add).then_inc(pooled_s, 1)

            def half_sums(b, h):
                dve.wait_ge(pooled_s, b * TILES + (h + 1) * HALF)
                dve.tensor_reduce(sums[:, h, :], pooled[:, h, :, :], AX.X, ALU.add)\
                    .then_inc(sums_ready, 1)

            def half_dev(b, h):
                dve.wait_ge(group_mean, 2 * b + h + 1)
                dve.tensor_tensor(dev, mean_c, bank(7)[:, 256:256 + HALF], ALU.subtract)\
                    .then_inc(dev_ready, 1)

            def half_var(b, h):
                dve.wait_ge(group_var, 2 * b + h + 1)
                dve.tensor_scalar(v_eps, bank(7)[:, 256:256 + HALF], 1.0, EPS_GN, ALU.mult, ALU.add)\
                    .then_inc(var_ready, 1)

            def round_max(a, k, first_bank=3):
                n = a * ROUNDS + k
                dve.wait_ge(scored, n + 1)
                if k > 1:
                    dve.wait_ge(exp_done, n - 1)
                dve.tensor_reduce(neg_max[:, k % 2, :], bank(first_bank, 2).rearrange("p (g m) -> p g m", m=POS),
                                  AX.X, ALU.max, negate=True).then_inc(max_ready, 1)

            def round_copy(a, k):
                n = a * ROUNDS + k
                dve.wait_ge(e_turned, n + 1)
                if k > 0:
                    dve.wait_ge(mixed, n)
                dve.tensor_copy(scratch[:, 1024:2048], bank(5, 2)).then_inc(e_copied, 1)

            def last_heads():
                for k in range(ROUNDS):
                    round_max(B - 1, k, LAST_BANK[k])
                    if k > 0:
                        round_copy(B - 1, k - 1)
                round_copy(B - 1, ROUNDS - 1)

            def means():
                dve.wait_ge(att_copied, B)
                for cc in range(CC):
                    dve.tensor_reduce(cov[:, cc, TD:TD + 1], mu[:, :, cc], AX.X, ALU.add)
                dve.drain()
                for cc in range(CC):
                    dve.tensor_scalar(cov[:, cc, TD:TD + 1], cov[:, cc, TD:TD + 1], 1.0 / (B * POS),
                                      None, ALU.mult)
                    dve.tensor_scalar(mu_d[:, cc, :], mu[:, :, cc], 1.0 / POS, None, ALU.mult)
                dve.drain()
                for cc in range(CC):
                    last = dve.tensor_scalar(mu_d[:, cc, :], mu_d[:, cc, :], cov[:, cc, TD:TD + 1],
                                             1.0 / float(np.sqrt(B)), ALU.subtract, ALU.mult)
                last.then_inc(mu_ready, 1)

            def qk_norms(a):
                dve.wait_ge(qk_squared, a + 1)
                dve.tensor_reduce(norm2, qk_sq.rearrange("p (g d) -> p g d", d=DH), AX.X, ALU.add)
                dve.drain()
                dve.tensor_scalar(norm2, norm2, EPS_NORM ** 2, None, ALU.max)\
                    .then_inc(norm_ready, 1)

            def copy_v(a):
                dve.wait_ge(qkv_part, TILES * (a + 1))
                dve.tensor_copy(v_sb, bank(2).rearrange("p (l n) -> p l n", l=LC))

            def qk_scale(a):
                dve.wait_ge(norm_root, a + 1)
                dve.reciprocal(rnorm, rnorm)
                dve.drain()
                r4 = rnorm.rearrange("p (l s h) -> p l s h", l=LC, s=2)
                for lc in range(LC):
                    dve.tensor_tensor(r4[:, lc, 1, :], r4[:, lc, 1, :], temp[:, :], ALU.mult)
                dve.drain()
                dve.tensor_tensor(
                    scratch[:, 1024:2048].rearrange("p (g d) -> p g d", d=DH),
                    bank(0, 2).rearrange("p (g d) -> p g d", d=DH),
                    rnorm.unsqueeze(2).to_broadcast([P, 2 * LC * HEADS, DH]), ALU.mult)\
                    .then_inc(qk_scaled, 1)

            def output_copy(c):
                dve.wait_ge(mixed, (c + 1) * ROUNDS)
                dve.tensor_copy(o_sb, bank(7).rearrange("p (c n) -> p c n", c=CC))\
                    .then_inc(o_copied, 1)
                dve.wait_ge(exp_done, (c + 1) * ROUNDS)
                dve.reciprocal(row_inv[:, :, :], row_sum[:, :, :])
                dve.drain()

            def normalise(c):
                dve.wait_ge(o_turned, c + 1)
                dve.tensor_tensor(
                    scratch[:, 2048:2560].rearrange("p (g d) -> p g d", d=DH),
                    bank(5).rearrange("p (g d) -> p g d", d=DH),
                    row_inv[:, :, :].rearrange("p l h -> p (l h)").unsqueeze(2)
                    .to_broadcast([P, LC * HEADS, DH]), ALU.mult).then_inc(at_ready, 1)

            def centre(c):
                dve.wait_ge(at_mean, c + 1)
                dve.tensor_tensor(a_c, a_t, bank(3)[:, 0:TD].unsqueeze(1)
                                  .to_broadcast([P, LC, TD]), ALU.subtract)\
                    .then_inc(ac_ready, 1)

            def add_cov(c):
                dve.wait_ge(cov_done, c + 1)
                dve.tensor_tensor(cov_sum[:, :, :], cov_sum[:, :, :], bank(3).rearrange(
                    "p (c n) -> p c n", c=CC), ALU.add).then_inc(cov_added, 1)

            def body(b, tiles, at, rest):
                a, c = b - 1, b - 2
                heads = rest and at
                if heads:
                    round_max(c, 1)
                if tiles:
                    pool_tile(b, 0)
                if tiles and not at:
                    wp_copy(0)
                if heads:
                    round_copy(c, 0)
                    round_max(c, 2)
                if at:
                    half_dev(a, 1)
                if heads:
                    round_copy(c, 1)
                if at:
                    half_var(a, 1)
                if heads:
                    round_max(c, 3)
                    round_copy(c, 2)
                if tiles:
                    pool_tile(b, 1)
                    if not at:
                        wp_copy(1)
                    pool_tile(b, 2)
                    if not at:
                        wp_copy(2)
                if heads:
                    round_copy(c, 3)
                if tiles:
                    pool_tile(b, 3)
                    if not at:
                        wp_copy(3)
                if rest:
                    output_copy(c)
                if tiles:
                    half_sums(b, 0)
                if rest:
                    normalise(c)
                if tiles:
                    half_dev(b, 0)
                if at:
                    qk_norms(a)
                    if tiles:
                        copy_v(a)
                    else:
                        qk_scale(a)
                if rest:
                    centre(c)
                if rest and not at:
                    means()
                    dve.wait_ge(mu_turned, 1)
                    dve.tensor_copy(mu_dt, bank(0)[0:B, 0:TD]).then_inc(mu_copied, 1)
                if tiles:
                    half_var(b, 0)
                    pool_tile(b, 4)
                if at and tiles:
                    qk_scale(a)
                if rest:
                    add_cov(c)
                if at and not tiles:
                    copy_v(a)
                if tiles:
                    pool_tile(b, 5)
                if at and tiles:
                    round_max(a, 0)
                if tiles:
                    pool_tile(b, 6)
                    pool_tile(b, 7)
                    half_sums(b, 1)

            dve.wait_ge(set_up, 6)
            dve.wait_ge(small_landed, 48)
            bodies(dve, body, last_heads)

            dve.wait_ge(mu_outer, 1)
            dve.wait_ge(cov_added, B)
            dve.tensor_tensor(cov[:, :, 0:TD], cov_sum[:, :, :], bank(1).rearrange(
                "p (c n) -> p c n", c=CC), ALU.add).then_inc(cov_ready, 1)

            def variances(h):
                for i in range(HALF):
                    n, o = h * HALF + i, BN_FIRST[h] + i
                    dve.wait_ge(cov_w, n + 1)
                    wait(dve, bn_read, n - 1)
                    dve.tensor_copy(bn_mean[:, o:o + 1], bank(2 + 2 * h + i)[:, TD:TD + 1])
                    dve.tensor_tensor_reduce(
                        out=prod[:, i % 2, :], in0=bank(2 + 2 * h + i)[:, 0:TD], in1=wp_n[:, o, :],
                        scale=1.0, scalar=0.0, op0=ALU.mult, op1=ALU.add,
                        accum_out=bn_var[:, o:o + 1]).then_inc(bn_read, 1)
                dve.wait_ge(bn_read, (h + 1) * HALF)
                cols = slice(BN_FIRST[h], BN_FIRST[h] + HALF)
                dve.tensor_scalar(bn_var[:, cols], bn_var[:, cols], 0.0, EPS_BN, ALU.max, ALU.add)\
                    .then_inc(bn_var_ready, 1)

            def scale_shift(h):
                cols = slice(BN_FIRST[h], BN_FIRST[h] + HALF)
                dve.wait_ge(bn_rstd_ready, h + 1)
                dve.tensor_tensor(bn_scale[:, cols], bn_rstd[:, cols], gam[:, cols], ALU.mult)
                dve.drain()
                dve.tensor_tensor(bn_mean[:, cols], bn_mean[:, cols], bn_scale[:, cols], ALU.mult)
                dve.drain()
                dve.tensor_tensor(bn_shift[:, cols], bet[:, cols], bn_mean[:, cols],
                                  ALU.subtract).then_inc(bn_ready, 1)


            variances(0)
            scale_shift(0)

            def add_item(k):
                for s in range(SLOTS):
                    if s < HALF:
                        dve.wait_ge(x_landed[s], (k + 2 * B) * 16)
                    else:
                        dve.wait_ge(x_landed[s], (k + 1) * 16)
                    for u in range(UNITS):
                        if isinstance(k, int) and s == 0 and u == 2:
                            variances(1)
                            scale_shift(1)
                        dve.wait_ge(scaled, (k * SLOTS + s) * UNITS + u + 1)
                        part = slots[:, s, u * UNIT:(u + 1) * UNIT]
                        dve.tensor_tensor(part, part, bank(2 * u, 2), ALU.add).then_inc(added, 1)

            add_item(0)
            with dve.Fori(1, B) as k:
                add_item(k)

        @block.tensor
        def _(pe):
            pe.wait_ge(con_landed, 16)
            pe.wait_ge(wq_landed, 16)
            for j in range(TILES):
                if j >= 2:
                    pe.wait_ge(w_copied, j - 1)
                for o in range(6):
                    last = pe.transpose(bank(2 * (j % 2), 2)[:, o * P:(o + 1) * P],
                                        w_stage[:, o, j * P:(j + 1) * P], ident)
                last.then_inc(w_turned, 1)
            pe.wait_ge(wp_landed, 16)
            for n in range(2 * CC):
                if n >= 2:
                    pe.wait_ge(wp_copied, n - 1)
                cc, g = divmod(n, 2)
                for o in range(4):
                    last = pe.transpose(bank(4 + n % 2)[:, o * P:(o + 1) * P],
                                        wp_n[:, 4 * g + o, cc * P:(cc + 1) * P], ident)
                last.then_inc(wp_turned, 1)
            pe.wait_ge(set_up, 6)
            pe.wait_ge(w_copied, TILES)
            pe.wait_ge(wp_copied, 2 * CC)

            def group_means(b, h):
                pe.wait_ge(mean_ready, 2 * b + h + 1)
                pe.matmul(bank(7)[:, 256:256 + HALF], lhsT=group, rhs=mean_c, start=True,
                          stop=True, skip_group_check=True).then_inc(group_mean, 1)

            def group_vars(b, h):
                pe.wait_ge(sq_ready, 2 * b + h + 1)
                pe.matmul(bank(7)[:, 256:256 + HALF], lhsT=group, rhs=sq_c, start=True,
                          stop=True, skip_group_check=True).then_inc(group_var, 1)

            def qkv(b, j, qk=True, v=True):
                h, i = divmod(j, HALF)
                if i == 0:
                    pe.wait_ge(xn_ready, 2 * b + h + 1)
                if j == 0:
                    wait(pe, qk_scaled, b)
                for lc in range(LC):
                    lhs = pooled[:, h, i, lc * P:(lc + 1) * P]
                    if qk:
                        done = pe.matmul(bank(lc), lhsT=lhs, rhs=w_t[:, j, 0:2 * TD],
                                         start=(j == 0), stop=(j == TILES - 1),
                                         skip_group_check=True)
                        if j == TILES - 1 and lc == LC - 1:
                            done.then_inc(qk_part, 1)
                    if v:
                        last = pe.matmul(bank(2)[:, lc * TD:(lc + 1) * TD], lhsT=lhs,
                                         rhs=w_t[:, j, 2 * TD:3 * TD], start=(j == 0 and lc == 0),
                                         stop=(j == TILES - 1), skip_group_check=True)
                if v:
                    last.then_inc(qkv_part, 1)

            def scores(a, k, before, first_bank=3, last_item=False):
                n = a * ROUNDS + k
                if k == 0:
                    pe.wait_ge(qk_copied, a + 1)
                    if before:
                        pe.wait_ge(cov_added, a)
                elif first_bank == 3:
                    pe.wait_ge(exp_done, n - 1 if last_item else n)
                elif k > 1:
                    pe.wait_ge(exp_done, n - 1)
                for u in range(2):
                    cc, g = divmod(2 * k + u, P // DH)
                    for lc in range(LC):
                        last = pe.matmul(bank(first_bank + u)[:, lc * POS:(lc + 1) * POS],
                                         lhsT=q_m[:, cc, g, lc * P:(lc + 1) * P],
                                         rhs=k_t[:, cc, :], start=True, stop=True,
                                         skip_group_check=True)
                last.then_inc(scored, 1)

            def turn_e(a, k):
                n = a * ROUNDS + k
                pe.wait_ge(exp_done, n + 1)
                if k > 0:
                    pe.wait_ge(e_copied, n)
                for u in range(2):
                    for lc in range(LC):
                        for mc in range(LC):
                            last = pe.transpose(
                                bank(5 + u)[:, mc * POS + lc * P:mc * POS + (lc + 1) * P],
                                e_sb[:, u, lc, mc * P:(mc + 1) * P], ident)
                last.then_inc(e_turned, 1)

            def mix(a, k):
                pe.wait_ge(e_copied, a * ROUNDS + k + 1)
                for u in range(2):
                    hd = 2 * k + u
                    cc, r = divmod(hd * DH, P)
                    for mc in range(LC):
                        last = pe.matmul(bank(7)[r:r + DH, cc * POS:(cc + 1) * POS],
                                         lhsT=v_sb[:, mc, hd * DH:(hd + 1) * DH],
                                         rhs=e_t[:, u, mc, :], start=(mc == 0),
                                         stop=(mc == LC - 1), skip_group_check=True)
                last.then_inc(mixed, 1)

            def last_heads():
                a = B - 1
                scores(a, 0, True)
                scores(a, 1, True, LAST_BANK[1], True)
                for k in range(ROUNDS):
                    turn_e(a, k)
                    if k + 2 < ROUNDS:
                        scores(a, k + 2, True, LAST_BANK[k + 2], True)
                    mix(a, k)

            def project(n, s, fresh):
                o = (s + 4) % TILES
                if fresh is not None:
                    pe.wait_ge(att_now_ready, fresh)
                wait(pe, added, (n - 1) * UNITS)
                wait(pe, low_copied, n)
                for w, row in enumerate(WINDOWS):
                    for cc in range(CC):
                        last = pe.matmul(bank(6)[:, w * P:(w + 1) * P],
                                         lhsT=att_now[:, cc, row * LOW:row * LOW + P],
                                         rhs=wp_t[:, cc, o * P:(o + 1) * P], start=(cc == 0),
                                         stop=(cc == CC - 1), skip_group_check=True)
                last.then_inc(low_done, 1)

            def turn_output(c):
                pe.wait_ge(o_copied, c + 1)
                for lc in range(LC):
                    for cc in range(CC):
                        last = pe.transpose(bank(5)[:, lc * TD + cc * P:lc * TD + (cc + 1) * P],
                                            o_sb[:, cc, lc * P:(lc + 1) * P], ident)
                last.then_inc(o_turned, 1)

            def turn_back(c):
                pe.wait_ge(at_ready, c + 1)
                for lc in range(LC):
                    last = pe.matmul(bank(3)[:, 0:TD], lhsT=ones[:, :], rhs=a_t[:, lc, :],
                                     start=(lc == 0), stop=(lc == LC - 1))
                last.then_inc(at_mean, 1)
                for cc in range(CC):
                    for lc in range(LC):
                        last = pe.transpose(bank(6)[:, cc * POS + lc * P:cc * POS + (lc + 1) * P],
                                            a_t[:, lc, cc * P:(cc + 1) * P], ident)
                last.then_inc(at_turned, 1)

            def gram_product(c):
                pe.wait_ge(ac_ready, c + 1)
                for lo in range(LC):
                    for lc in range(LC):
                        last = pe.matmul(bank(4)[:, lo * TD:(lo + 1) * TD],
                                         lhsT=gram[:, lc, lo * P:(lo + 1) * P],
                                         rhs=a_c[:, lc, :], start=(lc == 0),
                                         stop=(lc == LC - 1), skip_group_check=True)
                last.then_inc(gram_done, 1)

            def covariance(c):
                pe.wait_ge(gram_copied, c + 1)
                for cc in range(CC):
                    for lc in range(LC):
                        last = pe.matmul(bank(3)[:, cc * TD:(cc + 1) * TD],
                                         lhsT=a_c[:, lc, cc * P:(cc + 1) * P],
                                         rhs=g_sb[:, lc, :], start=(lc == 0),
                                         stop=(lc == LC - 1), skip_group_check=True)
                last.then_inc(cov_done, 1)

            def turn_qk(a, rest):
                pe.wait_ge(qk_scaled, a + 1)
                if rest:
                    pe.wait_ge(att_copied, a)
                for s in range(2):
                    for cc in range(CC):
                        for lc in range(LC):
                            last = pe.transpose(
                                bank(5 + s)[:, cc * POS + lc * P:cc * POS + (lc + 1) * P],
                                qk_n[:, lc, s * TD + cc * P:s * TD + (cc + 1) * P], ident)
                last.then_inc(qk_turned, 1)

            def turn_means():
                pe.wait_ge(mu_ready, 1)
                for cc in range(CC):
                    last = pe.transpose(bank(0)[0:B, cc * P:(cc + 1) * P], mu_d[:, cc, :], ident)
                last.then_inc(mu_turned, 1)

            def means_product():
                pe.wait_ge(mu_copied, 1)
                for cc in range(CC):
                    last = pe.matmul(bank(1)[:, cc * TD:(cc + 1) * TD],
                                     lhsT=mu_dt[:, cc * P:(cc + 1) * P], rhs=mu_dt,
                                     start=True, stop=True, skip_group_check=True)
                last.then_inc(mu_outer, 1)

            def body(b, tiles, at, rest):
                a, c = b - 1, b - 2
                heads = rest and at
                if heads:
                    scores(c, 1, True)
                    turn_e(c, 0)
                if at:
                    qkv(a, 3)
                if heads:
                    scores(c, 2, True)
                    turn_e(c, 1)
                    mix(c, 0)
                if at:
                    group_means(a, 1)
                    group_vars(a, 1)
                if heads:
                    scores(c, 3, True)
                    turn_e(c, 2)
                    pe.wait_ge(var_ready, 2 * a + 2)
                    mix(c, 1)
                if at:
                    qkv(a, 4, v=tiles)
                    qkv(a, 5, v=tiles)
                if heads:
                    mix(c, 2)
                    turn_e(c, 3)
                if at:
                    qkv(a, 6, v=tiles)
                if heads:
                    mix(c, 3)
                if at:
                    qkv(a, 7, v=tiles)
                if rest:
                    turn_output(c)
                if at and not tiles:
                    for j in range(HALF, TILES):
                        qkv(a, j, qk=False)
                if tiles:
                    group_means(b, 0)
                if rest:
                    turn_back(c)
                if tiles:
                    group_vars(b, 0)
                if rest:
                    gram_product(c)
                    if not at:
                        turn_means()
                if at and not tiles:
                    turn_qk(a, rest)
                if rest:
                    covariance(c)
                    if not at:
                        means_product()
                        project(0, 0, 1)
                if at and tiles:
                    turn_qk(a, rest)
                if tiles:
                    qkv(b, 0)
                if at and tiles:
                    scores(a, 0, rest)
                if tiles:
                    qkv(b, 1)
                    qkv(b, 2)

            bodies(pe, body, last_heads)

            pe.wait_ge(cov_ready, 1)

            def channel_products(h):
                for i in range(HALF):
                    o = BN_FIRST[h] + i
                    for cc in range(CC):
                        last = pe.matmul(bank(2 + 2 * h + i)[:, 0:TD + 1],
                                         lhsT=wp_t[:, cc, o * P:(o + 1) * P], rhs=cov[:, cc, :],
                                         start=(cc == 0), stop=(cc == CC - 1))
                    last.then_inc(cov_w, 1)

            channel_products(0)

            def upsample_item(k, last_item):
                for s in range(SLOTS):
                    n = k * SLOTS + s
                    pe.wait_ge(low_copied, n + 1)
                    for u in range(UNITS):
                        if isinstance(k, int) and k == 0 and s == 0 and u == 1:
                            pe.wait_ge(bn_read, HALF)
                        if isinstance(k, int) and k == 0 and s == 0 and u == 2:
                            channel_products(1)
                            pe.wait_ge(bn_read, TILES)
                        if u == 2 and s < SLOTS - 1:
                            project(n + 1, s + 1, None)
                        elif u == 2 and not last_item:
                            project(n + 1, 0, k + 2)
                        wait(pe, added, (n - 1) * UNITS + u + 1)
                        if u == 3 and not (last_item and s == SLOTS - 1):
                            pe.wait_ge(low_copied, n + 2)
                        for v in range(2):
                            blk = 2 * u + v
                            last = pe.matmul(bank(blk), lhsT=low_t[:, s % 2, WINDOW_OF[blk], :],
                                             rhs=up[:, blk * 8:(blk + 1) * 8, :], start=True,
                                             stop=True)
                        last.then_inc(upsampled, 1)

            pe.wait_ge(up_ready, 2)
            upsample_item(0, False)
            with pe.Fori(1, B - 1) as k:
                upsample_item(k, False)
            upsample_item(B - 1, True)


_INS = ["x", "L0_conv_w_qkv", "L0_conv_temperature", "L0_conv_w_proj", "L0_conv_bn_gamma",
        "L0_conv_bn_beta"]


def kernel(**inputs):
    import concourse.bacc as bacc
    from concourse.bass_utils import run_bass_kernel_spmd

    nc = bacc.Bacc("TRN2", target_bir_lowering=False, num_devices=1)
    arrays, args = {}, []
    for name in _INS:
        a = np.ascontiguousarray(inputs[name])
        arrays[f"in_{name}"] = a
        args.append(nc.dram_tensor(f"in_{name}", a.shape, mybir.dt.from_np(a.dtype),
                                   kind="ExternalInput").ap())
    table = constants()
    arrays["tables"] = table
    tab = nc.dram_tensor("tables", table.shape, F32, kind="ExternalInput").ap()
    out = nc.dram_tensor("out", (B, CH, H, W), F32, kind="ExternalOutput").ap()
    program(nc, *args, tab, out)
    r = run_bass_kernel_spmd(nc, [arrays], core_ids=[0])
    return r.results[0]["out"]
```
